# Optimizing a Trainium2 kernel written in Bass

```python
import numpy as np
import jax
import jax.numpy as jnp

def _softmax(x, axis=-1):
    return jax.nn.softmax(x, axis=axis)

def _gelu(x):
    return jax.nn.gelu(x, approximate=True)

def _silu(x):
    return jax.nn.silu(x)

def _sigmoid(x):
    return jax.nn.sigmoid(x)

def _layernorm(x, axis=-1, eps=1e-05):
    m = jnp.mean(x, axis=axis, keepdims=True)
    v = jnp.var(x, axis=axis, keepdims=True)
    return (x - m) / jnp.sqrt(v + eps)

def _scatter_add(tgt, idx, src, axis=0):
    return tgt.at[idx].add(src)

def _segment_sum(src, seg, n):
    return jax.ops.segment_sum(src, seg, n)
kernel_name = 'mk_adj_ffn_d1_adj_r2_be54ae'

def setup_inputs(seed: int=0):
    np.random.seed(seed)
    _w = jnp.asarray

    def _rec_inputs():
        import jax
        import jax.numpy as jnp
        _gk = jax.random.key(seed)
        x = -0.000125 + 0.9999 * jax.random.normal(jax.random.fold_in(_gk, 1), (16, 512, 256), jnp.float32)
        _a = jax.random.bernoulli(jax.random.fold_in(_gk, 2), 0.015625, (512, 512))
        _a = jnp.logical_or(_a, jnp.swapaxes(_a, -1, -2))
        _a = jnp.logical_or(_a, jnp.eye(512, dtype=bool))
        _af = _a.astype(jnp.float32)
        adj = _af
        return (x, adj)
    x, adj = _rec_inputs()

    def _L0_gnn_setup():
        import jax, jax.numpy as jnp
        import numpy as np
        ALPHA = 0.2
        key = jax.random.key(seed)
        k0, k1, k2, k3 = jax.random.split(key, 4)
        B, N, C, F = (64, 512, 256, 256)
        x = jax.random.normal(k0, (B, N, C), dtype=jnp.float32)
        W = jax.random.normal(k1, (C, F), dtype=jnp.float32) * (1.414 / np.sqrt(C + F))
        a = jax.random.normal(k2, (2 * F, 1), dtype=jnp.float32) * (1.414 / np.sqrt(2 * F + 1))
        beta = jnp.ones((1,), dtype=jnp.float32)
        mask = (jax.random.uniform(k3, (N, N)) < 0.3).astype(jnp.float32)
        return {'x': x, 'W': W, 'a': a, 'beta': beta, 'mask': mask}
    _L0_gnn_all = _L0_gnn_setup()
    _L0_gnn_in = {k: v for k, v in _L0_gnn_all.items() if k in ('W', 'a', 'beta')}
    del _L0_gnn_all

    def _L0_ffn_setup():
        import jax, jax.numpy as jnp
        import numpy as np
        B, S, D, DFF, E, K = (4, 1024, 256, 512, 8, 2)
        key = jax.random.key(seed)
        ks = jax.random.split(key, 5)
        x = jax.random.normal(ks[0], (B, S, D), dtype=jnp.float32)
        Wg = jax.random.normal(ks[1], (D, E), dtype=jnp.float32) * 0.02
        bg = jnp.zeros((E,), dtype=jnp.float32)
        W1 = jax.random.normal(ks[2], (E, D, 2 * DFF), dtype=jnp.float32) * 0.02
        b1 = jnp.zeros((E, 2 * DFF), dtype=jnp.float32)
        W2 = jax.random.normal(ks[3], (E, DFF, D), dtype=jnp.float32) * 0.02
        b2 = jnp.zeros((E, D), dtype=jnp.float32)
        return {'x': x, 'Wg': Wg, 'bg': bg, 'W1': W1, 'b1': b1, 'W2': W2, 'b2': b2}
    _L0_ffn_all = _L0_ffn_setup()
    _L0_ffn_in = {k: v for k, v in _L0_ffn_all.items() if k in ('Wg', 'bg', 'W1', 'b1', 'W2', 'b2')}
    del _L0_ffn_all
    return {'x': x, 'adj': adj, 'L0_gnn_W': _L0_gnn_in['W'], 'L0_gnn_a': _L0_gnn_in['a'], 'L0_gnn_beta': _L0_gnn_in['beta'], 'L0_ffn_Wg': _L0_ffn_in['Wg'], 'L0_ffn_bg': _L0_ffn_in['bg'], 'L0_ffn_W1': _L0_ffn_in['W1'], 'L0_ffn_b1': _L0_ffn_in['b1'], 'L0_ffn_W2': _L0_ffn_in['W2'], 'L0_ffn_b2': _L0_ffn_in['b2']}

def reference(x, adj, L0_gnn_W, L0_gnn_a, L0_gnn_beta, L0_ffn_Wg, L0_ffn_bg, L0_ffn_W1, L0_ffn_b1, L0_ffn_W2, L0_ffn_b2):
    import jax
    import jax.numpy as jnp

    def _L0_gnn_ref(x, W, a, beta, mask):
        import jax, jax.numpy as jnp
        import numpy as np
        ALPHA = 0.2
        F_ = W.shape[1]
        h = jnp.einsum('bnc,cf->bnf', x, W)
        a1, a2 = (a[:F_, 0], a[F_:, 0])
        s1 = jnp.einsum('bnf,f->bn', h, a1)
        s2 = jnp.einsum('bnf,f->bn', h, a2)
        e = jax.nn.leaky_relu(s1[:, :, None] + s2[:, None, :], negative_slope=ALPHA)
        e = e * mask[None, :, :]
        att = jax.nn.softmax(e, axis=2)
        h_prime = jnp.einsum('bij,bjf->bif', att, h)
        return jax.nn.elu(h_prime + beta * h)

    def _L0_ffn_ref(x, Wg, bg, W1, b1, W2, b2):
        import jax, jax.numpy as jnp
        import numpy as np
        B, S, D, DFF, E, K = (4, 1024, 256, 512, 8, 2)
        n_experts = W1.shape[0]
        logits = jnp.einsum('bsd,de->bse', x, Wg) + bg
        topk_vals, topk_idx = jax.lax.top_k(logits, K)
        topk_w = jax.nn.softmax(topk_vals, axis=-1)
        one_hot = jax.nn.one_hot(topk_idx, n_experts, dtype=x.dtype)
        weights_per_expert = jnp.einsum('bske,bsk->bse', one_hot, topk_w)
        h = jnp.einsum('bsd,edf->bsef', x, W1) + b1
        a, g = jnp.split(h, 2, axis=-1)
        act = jax.nn.silu(a) * g
        expert_out = jnp.einsum('bsef,efd->bsed', act, W2) + b2
        return jnp.einsum('bse,bsed->bsd', weights_per_expert, expert_out)
    x = x + _L0_gnn_ref(_layernorm(x, axis=-1), L0_gnn_W, L0_gnn_a, L0_gnn_beta, adj)
    x = x + _L0_ffn_ref(_layernorm(x, axis=-1), L0_ffn_Wg, L0_ffn_bg, L0_ffn_W1, L0_ffn_b1, L0_ffn_W2, L0_ffn_b2)
    return x

_drawn_inputs = setup_inputs


def setup_inputs(seed=0):
    import zlib

    import numpy as np

    out = dict(_drawn_inputs(seed))
    spreads = {'L0_ffn_bg': (0.0, 0.301), 'L0_ffn_b1': (0.0, 0.8), 'L0_ffn_b2': (0.0, 0.1)}
    factors = {'L0_ffn_W1': 3.885, 'L0_ffn_W2': 3.853}
    for name, (base, spread) in spreads.items():
        noise = np.random.default_rng([zlib.crc32(name.encode()), seed]).standard_normal(out[name].shape)
        drawn = base * np.exp(spread * noise) if base else spread * noise
        out[name] = jnp.asarray(drawn.astype(out[name].dtype))
    for name, factor in factors.items():
        out[name] = (out[name] * factor).astype(out[name].dtype)
    return out
```

```python
from contextlib import ExitStack

import concourse.bass as bass
from concourse import mybir

F32 = mybir.dt.float32
F16 = mybir.dt.float16
BF16 = mybir.dt.bfloat16
I32 = mybir.dt.int32
U32 = mybir.dt.uint32
ALU = mybir.AluOpType
ACT = mybir.ActivationFunctionType
AX = mybir.AxisListType.X

P = 128
T = 256
JT = T // P
SX = 16.0
SW = 64.0
SA = 16.0
EPS = 1e-5
ALPHA = 0.2


def put(value, least=1):
    return not isinstance(value, int) or value >= least


def wait(eng, semaphore, value):
    if put(value):
        eng.wait_ge(semaphore, value)


def build_gat_moe(nc, x, adj, gW, ga, gbeta, Wg, bg, W1, b1, W2, b2, out):
    B, N, C = x.shape
    NI = N // P
    KC = C // P
    E = Wg.shape[1]
    DFF = W2.shape[1]
    FA = DFF // P
    H1 = 2 * DFF
    MT = H1 // P
    KF = DFF // P
    TOK = B * N
    NG = B * NI
    NT = 2 * TOK // T + E - 1
    R = TOK + T
    NCH = E * KC
    assert NCH == B and KC == 2 and KF == 2 * KC and NT % 2 == 1

    x_v = x.rearrange("b (p n) c -> b p n c", n=NI)
    out_v = out.rearrange("b (p n) c -> b p n c", n=NI)
    adj_v = adj.rearrange("(p n) j -> p n j", n=NI)
    W1_v = W1.rearrange("e (k p) f -> (e k) p f", p=P)
    W2_v = W2.rearrange("e (a k p) c -> (e a) p k c", p=P, k=KC)

    rows_d = nc.dram_tensor("expert_rows", (E * R + T, 2 * C), F16, kind="Internal").ap()
    y_d = nc.dram_tensor("expert_results", (NT * T, C), F32, kind="Internal").ap()

    at = [(nc.sbuf_base + 31) // 32 * 32]

    def sb(name, shape, dt):
        size = mybir.dt.size(dt)
        for d in shape[1:]:
            size *= d
        t = nc.alloc_sbuf_tensor_at(name, list(shape), dt, offset=at[0])
        at[0] += (size + 31) // 32 * 32
        assert at[0] <= nc.sbuf_usable_end, (name, at[0])
        return t

    w1h = sb("w1h", [P, E * KC, H1], F16)
    w1l = sb("w1l", [P, E * KC, H1], F16)
    w2h = sb("w2h", [P, E * KF, C], F16)
    w2l = sb("w2l", [P, E * KF, C], F16)
    b1T = sb("b1T", [P, E * MT], F32)
    b1S = sb("b1S", [P, E * MT], F32)
    b2b = sb("b2b", [P, E, C], F32)
    rank_all = sb("rank_all", [P, B, 2 * NI], F32)
    exp_all = sb("exp_all", [P, B, 2 * NI], F32)
    dlg_all = sb("dlg_all", [P, B, NI], F32)
    macc = sb("macc", [P, E], BF16)
    ones16 = sb("ones16", [P, P], BF16)
    idh = sb("idh", [P, P], F16)
    phase = at[0]

    idf = sb("idf", [P, P], F32)
    onesf = sb("onesf", [P, P], F32)
    tri = sb("tri", [P, P], BF16)
    trif = sb("trif", [P, P], F32)
    wx = sb("wx", [P, KC, C + 1], F32)
    av = sb("av", [P, 2 * C], F32)
    wa2 = sb("wa2", [P, KC], F32)
    wa2r = sb("wa2r", [P, KC, P], F32)
    betat = sb("betat", [P, 1], F32)
    bgb = sb("bgb", [P, NI, E], F32)
    wg = sb("wg", [P, KC, E], F32)
    iota2 = sb("iota2", [P, 2 * NI, E], F32)
    halfs = sb("halfs", [P, NI], F32)
    mask = sb("mask", [P, NI, N], F32)
    wst1 = sb("wst1", [P, H1], F32)
    wst2 = sb("wst2", [P, KC, C], F32)
    xt = [sb(f"xt{i}", [P, NI, C], F32) for i in range(2)]
    xr = [sb(f"xr{i}", [P, NI, C], F32) for i in range(2)]
    xn = sb("xn", [P, NI, C], F32)
    xn2 = sb("xn2", [P, NI, C], F32)
    xT = sb("xT", [P, KC, N], F32)
    x2T = sb("x2T", [P, KC, N], F32)
    hs = [sb(f"hs{i}", [P, NI, C + 1], F32) for i in range(2)]
    zb = [sb(f"zb{i}", [P, NI, C], F32) for i in range(2)]
    ez = sb("ez", [P, NI, C], F32)
    at_s = [sb(f"at_s{i}", [P, N], F32) for i in range(2)]
    em = [sb(f"em{i}", [P, N], F32) for i in range(2)]
    pb = [sb(f"pb{i}", [P, N], F32) for i in range(2)]
    pT = [sb(f"pT{i}", [P, NI, P], F32) for i in range(2)]
    rows = [sb(f"rows{i}", [P, NI, 2 * C], F16) for i in range(2)]
    st1 = sb("st1", [P, NI, 6], F32)
    mv1 = sb("mv1", [P, NI, 2], F32)
    st2 = sb("st2", [P, NI, 6], F32)
    mv2 = sb("mv2", [P, NI, 2], F32)
    ve1 = sb("ve1", [P, NI], F32)
    ve2 = sb("ve2", [P, NI], F32)
    rs1 = sb("rs1", [P, NI], F32)
    rs2 = sb("rs2", [P, NI], F32)
    rmax = sb("rmax", [P, 2, 1], F32)
    nmax = sb("nmax", [P, 2, 1], F32)
    rsum = sb("rsum", [P, 4, 1], F32)
    rinv = sb("rinv", [P, 2, 1], F32)
    lg = sb("lg", [P, NI, E], F32)
    mx = sb("mx", [P, NI, E], F32)
    ix = sb("ix", [P, NI, E], U32)
    ixf = sb("ixf", [P, 2, NI], F32)
    oh = sb("oh", [P, 2 * NI, E], F32)
    m16 = sb("m16", [P, NI, E], BF16)
    msum = sb("msum", [P, E], F32)
    rk = sb("rk", [P, 2 * NI, E], F32)
    rkr = sb("rkr", [P, 2 * NI], F32)
    slot = [sb(f"slot{i}", [P, 2 * NI], I32) for i in range(2)]

    at[0] = phase
    xs = [sb(f"xs{i}", [P, JT, 2 * C], F16) for i in range(2)]
    xsT = [sb(f"xsT{i}", [P, 2 * KC, T], F16) for i in range(2)]
    sil = [sb(f"sil{i}", [P, T], F32) for i in range(2)]
    act = [sb(f"act{i}", [P, T], F32) for i in range(2)]
    ah = [sb(f"ah{i}", [P, KF, T], F16) for i in range(2)]
    al = [sb(f"al{i}", [P, KF, T], F16) for i in range(2)]
    ys = [sb(f"ys{i}", [P, JT, C], F32) for i in range(2)]
    zrow = sb("zrow", [P, JT, 2 * C], F16)
    cnt = sb("cnt", [P, E], F32)
    cnti = sb("cnti", [P, E], I32)
    cntp = sb("cntp", [P, E], I32)
    nti = sb("nti", [P, E], I32)
    ntf = sb("ntf", [P, E], F32)
    one8 = sb("one8", [P, E], F32)
    ends = sb("ends", [P, E], F32)
    base = sb("base", [P, E], F32)
    s_io = sb("s_io", [1, NT, E], F32)
    ge = sb("ge", [1, NT, E], F32)
    gn = sb("gn", [1, NT, E], F32)
    ex = sb("ex", [1, NT], F32)
    stt = sb("stt", [1, NT], F32)
    srow = sb("srow", [1, NT], F32)
    tabe = sb("tabe", [1, NT], I32)
    tabr = sb("tabr", [1, NT], I32)
    yf = sb("yf", [P, B, 2 * NI], F32)
    yi = sb("yi", [P, B, 2 * NI], I32)
    ybs = sb("ybs", [P, B, 2 * NI], F32)
    wk = sb("wk", [P, 2, NG], F32)
    gy = [sb(f"gy{i}", [P, 2, C], F32) for i in range(4)]
    xo = [sb(f"xo{i}", [P, NI, C], F32) for i in range(2)]

    with ExitStack() as ctx:
        bank = [ctx.enter_context(nc.psum_tensor(f"bank{i}", [P, 512], F32)) for i in range(8)]
        gate_ps = bank[3][:, 0:NI * E]
        rank_ps = bank[4][:, 0:NI * E]

        def sem(name):
            return ctx.enter_context(nc.semaphore(name))

        const_in = sem("const_in")
        x_in = [sem(f"x_in{i}") for i in range(2)]
        xr_in = [sem(f"xr_in{i}") for i in range(2)]
        w_in = sem("w_in")
        adj_in = sem("adj_in")
        x1_out = [sem(f"x1_out{i}") for i in range(2)]
        scattered = [sem(f"scattered{i}") for i in range(2)]
        consts = sem("consts")
        onesd = sem("onesd")
        wa_done = sem("wa_done")
        b1t_ps = sem("b1t_ps")
        b1t_sb = sem("b1t_sb")
        ln1_st = sem("ln1_st")
        ln1_mv = sem("ln1_mv")
        ve1_done = sem("ve1_done")
        rs1_done = sem("rs1_done")
        xn_done = sem("xn_done")
        t1_done = sem("t1_done")
        xT_sb = sem("xT_sb")
        h_ps = sem("h_ps")
        h_sb = sem("h_sb")
        s2_ps = sem("s2_ps")
        bh_done = sem("bh_done")
        a_done = sem("a_done")
        lr_done = sem("lr_done")
        em_done = sem("em_done")
        nm_done = sem("nm_done")
        p_done = sem("p_done")
        pt_ps = sem("pt_ps")
        pt_sb = sem("pt_sb")
        att_ps = sem("att_ps")
        ri_done = sem("ri_done")
        z_done = sem("z_done")
        ez_done = sem("ez_done")
        rl_done = sem("rl_done")
        x1_done = sem("x1_done")
        ln2_st = sem("ln2_st")
        ln2_mv = sem("ln2_mv")
        ve2_done = sem("ve2_done")
        rs2_done = sem("rs2_done")
        xn2_done = sem("xn2_done")
        hi_done = sem("hi_done")
        lo_done = sem("lo_done")
        t2_done = sem("t2_done")
        x2T_sb = sem("x2T_sb")
        gate_done = sem("gate_done")
        lg_done = sem("lg_done")
        mx_done = sem("mx_done")
        ix_done = sem("ix_done")
        ixf_done = sem("ixf_done")
        oh_done = sem("oh_done")
        m_done = sem("m_done")
        rank_done = sem("rank_done")
        msum_done = sem("msum_done")
        macc_done = sem("macc_done")
        rk_done = sem("rk_done")
        rkr_done = sem("rkr_done")
        slot_done = sem("slot_done")
        whi_done = sem("whi_done")
        wsc_done = sem("wsc_done")
        wlo_done = sem("wlo_done")
        cnt_ps = sem("cnt_ps")
        tb = sem("tb")
        table = sem("table")
        zdone = sem("zdone")
        zmem = sem("zmem")
        xs_in = [sem(f"xs_in{i}") for i in range(2)]
        xst_ps = sem("xst_ps")
        xst_sb = sem("xst_sb")
        ag_ps = sem("ag_ps")
        sil_done = sem("sil_done")
        act_done = sem("act_done")
        ah_done = sem("ah_done")
        al_done = sem("al_done")
        y_ps = sem("y_ps")
        y_sb = sem("y_sb")
        y_out = [sem(f"y_out{i}") for i in range(2)]
        yi_done = sem("yi_done")
        wk_done = sem("wk_done")
        ed_done = sem("ed_done")
        cw = sem("cw")
        gy_in = [sem(f"gy_in{i}") for i in range(4)]
        xo_in = [sem(f"xo_in{i}") for i in range(2)]
        c1_done = sem("c1_done")
        c2_done = sem("c2_done")
        fin_out = [sem(f"fin_out{i}") for i in range(2)]

        NCONST = 10
        block = ctx.enter_context(nc.Block())

        LAGS = 5
        LAST = B + LAGS - 1

        def graph_steps(eng, step, tail=0):
            def one(i):
                step([((i - lag) // 2, (i - lag) % 2) if 0 <= i - lag < B else None for lag in range(LAGS)])
            for i in range(6):
                one(i)
            with eng.Fori(3, (B - tail) // 2) as j:
                for u in range(2):
                    step([(j + (u - lag) // 2, (u - lag) % 2) for lag in range(LAGS)])
            for i in range(B - tail, LAST):
                one(i)

        def tile_at(G, t, lag):
            g = G[1] if t >= lag else G[2]
            return g and (g, (t - lag) % NI)

        @block.sync
        def _(sp):
            sp.dma_start(xt[0][:, :, :], x_v[0]).then_inc(x_in[0], 16)
            sp.dma_start(wx[:, :, 0:C], gW.rearrange("(k p) f -> p k f", p=P)).then_inc(const_in, 16)
            sp.dma_start(av[:, :], ga.rearrange("f o -> (f o)").partition_broadcast(P)).then_inc(const_in, 16)
            sp.dma_start(betat[:, :], gbeta.partition_broadcast(P)).then_inc(const_in, 16)
            sp.dma_start(wg[:, :, :], Wg.rearrange("(k p) e -> p k e", p=P)).then_inc(const_in, 16)
            for n in range(NI):
                sp.dma_start(bgb[:, n, :], bg.partition_broadcast(P)).then_inc(const_in, 16)
            adj_nat = [xr[i][:, :, :].rearrange("p n c -> p (n c)").rearrange("p (n j) -> p n j", j=N) for i in range(2)]
            for i in range(2):
                sp.dma_start(adj_nat[i], adj_v[:, 2 * i:2 * i + 2, :]).then_inc(adj_in, 16)
            sp.dma_start(xn2[0:E * MT, 0, 0:P], b1.rearrange("e (m p) -> (e m) p", p=P)).then_inc(const_in, 16)
            sp.dma_start(b2b[:, :, :], b2.rearrange("e c -> (e c)").partition_broadcast(P)).then_inc(const_in, 16)

            def step(G):
                if G[0]:
                    q, s = G[0]
                    b = 2 * q + s
                    if not isinstance(b, int) or b + 1 < B:
                        wait(sp, xn_done, NI * b)
                        sp.dma_start(xt[1 - s][:, :, :], x_v[b + 1]).then_inc(x_in[1 - s], 16)
                    wait(sp, wlo_done, 2 * b)
                    sp.dma_start(wst1[:, :], W1_v[b]).then_inc(w_in, 16)
                    sp.dma_start(wst2[:, :, :], W2_v[b]).then_inc(w_in, 16)
                if G[3]:
                    q, s = G[3]
                    b = 2 * q + s
                    sp.wait_ge(x1_done, b + 1)
                    sp.dma_start(out_v[b], xr[s][:, :, :]).then_inc(x1_out[s], 16)
                if G[1]:
                    q, s = G[1]
                    b = 2 * q + s
                    if put(q):
                        sp.wait_ge(x1_out[s], 16 * q)
                        sp.wait_ge(xn2_done, (b - 1) * NI)
                    else:
                        sp.wait_ge(consts, 4)
                    sp.dma_start(xr[s][:, :, :], x_v[b]).then_inc(xr_in[s], 16)

            graph_steps(sp, step, tail=2)

            sp.wait_ge(zmem, 1)
            sp.dma_start(rows_d[E * R:E * R + T, :].rearrange("(p j) c -> p j c", j=JT), zrow[:, :, :]).then_inc(zdone, 16)
            sp.wait_ge(table, 1)
            for e in range(E):
                c_e = sp.value_load(cnti[0:1, e:e + 1], min_val=0, max_val=TOK)
                sp.dma_start(rows_d[bass.ds(c_e + e * R, T), :].rearrange("(p j) c -> p j c", j=JT), zrow[:, :, :]).then_inc(zdone, 16)
            sp.wait_ge(zdone, 16 * (E + 1))
            for s in range(2):
                sp.wait_ge(scattered[s], 16 * 2 * NI * (B // 2))
                sp.wait_ge(x1_out[s], 16 * (B // 2))

            def load_rows(t, s):
                r = sp.value_load(tabr[0:1, bass.ds(t, 1)], min_val=0, max_val=E * R)
                sp.dma_start(xs[s][:, :, :], rows_d[bass.ds(r, T), :].rearrange("(p j) c -> p j c", j=JT)).then_inc(xs_in[s], 16)

            def store_y(t, s):
                sp.wait_ge(y_sb, t + 1)
                sp.dma_start(y_d[bass.ds(t * T, T), :].rearrange("(p j) c -> p j c", j=JT), ys[s][:, :, :]).then_inc(y_out[s], 16)

            load_rows(0, 0)
            load_rows(1, 1)
            with sp.Fori(0, (NT - 3) // 2) as j:
                for s in range(2):
                    sp.wait_ge(xst_ps, 2 * j + s + 1)
                    load_rows(2 * j + s + 2, s)
                    store_y(2 * j + s, s)
            t = NT - 3
            sp.wait_ge(xst_ps, t + 1)
            load_rows(t + 2, 0)
            store_y(t, 0)
            store_y(t + 1, 1)
            store_y(t + 2, 0)
            sp.wait_ge(y_out[0], 16 * ((NT + 1) // 2))
            sp.wait_ge(y_out[1], 16 * (NT // 2))
            sp.sem_inc(cw, 1)
            for s in range(2):
                sp.dma_start(xo[s][:, :, :], out_v[s]).then_inc(xo_in[s], 16)
            with sp.Fori(0, B // 2 - 1) as j:
                for s in range(2):
                    sp.wait_ge(c2_done, 8 * j + 4 * s + 4)
                    sp.dma_start(out_v[2 * j + s], xo[s][:, :, :]).then_inc(fin_out[s], 16)
                for s in range(2):
                    sp.wait_ge(fin_out[s], 16 * j + 16)
                    sp.dma_start(xo[s][:, :, :], out_v[2 * j + s + 2]).then_inc(xo_in[s], 16)
            for s in range(2):
                sp.wait_ge(c2_done, NI * (B - 2 + s) + NI)
                sp.dma_start(out_v[B - 2 + s], xo[s][:, :, :]).then_inc(fin_out[s], 16)
            for s in range(2):
                sp.wait_ge(fin_out[s], 16 * (B // 2))

        @block.gpsimd
        def _(pool):
            pool.memset(onesf[:, :], 1.0).then_inc(onesd, 1)
            pool.memset(halfs[:, :], -0.5).then_inc(onesd, 1)
            pool.memset(macc[:, :], 0.0).then_inc(onesd, 1)
            pool.iota(iota2[:, :, :], pattern=[[0, 2 * NI], [1, E]], base=0, channel_multiplier=0, allow_small_or_imprecise_dtypes=True).then_inc(onesd, 1)
            pool.wait_ge(onesd, 4)
            pool.affine_select(idf[:, :], onesf[:, :], pattern=[[-1, P]], compare_op=ALU.is_equal, fill=0.0, base=0, channel_multiplier=1).then_inc(consts, 1)
            pool.affine_select(trif[:, :], onesf[:, :], pattern=[[1, P]], compare_op=ALU.is_gt, fill=0.0, base=0, channel_multiplier=-1).then_inc(consts, 1)
            adj_nat = [xr[i][:, :, :].rearrange("p n c -> p (n c)").rearrange("p (n j) -> p n j", j=N) for i in range(2)]
            pool.wait_ge(adj_in, 32)
            for n in range(NI):
                src = adj_nat[n // 2][:, n % 2, :].rearrange("p (q m) -> p m q", m=NI)
                i_ = pool.tensor_scalar(mask[:, n, :].rearrange("p (m q) -> p m q", m=NI), src, 1.0, 1.0, ALU.mult, ALU.mult)
                if n % 2:
                    i_.then_inc(consts, 1)
            pool.wait_ge(const_in, 16 * NCONST)

            def step(G):
                if G[1]:
                    q, s = G[1]
                    b = 2 * q + s
                    pool.wait_ge(h_sb, NI * b + NI)
                    wait(pool, rl_done, b - 1)
                    wait(pool, ez_done, b - 1)
                    pool.nop(nofuse=True)
                    pool.tensor_scalar(zb[s][:, :, :], hs[s][:, :, 0:C], betat[:, 0:1], -1.0, ALU.mult, ALU.add).then_inc(bh_done, 1)
                if G[0]:
                    q, s = G[0]
                    b = 2 * q + s
                    pool.wait_ge(ln1_mv, NI * b + NI)
                    pool.nop(nofuse=True)
                    pool.tensor_scalar(ve1[:, :], mv1[:, :, 1], 1.0, EPS, ALU.mult, ALU.add).then_inc(ve1_done, 1)
                    pool.wait_ge(ve1_done, b + 1)
                    wait(pool, xn_done, NI * b)
                    pool.tensor_tensor(rs1[:, :], ve1[:, :], halfs[:, :], ALU.pow).then_inc(rs1_done, 1)
                if G[0]:
                    q, s = G[0]
                    b = 2 * q + s
                    pool.wait_ge(whi_done, 2 * b + 2)
                    pool.nop(nofuse=True)
                    pool.tensor_scalar(wst1[:, :], wst1[:, :], SW, 1.0, ALU.mult, ALU.mult).then_inc(wsc_done, 1)
                    pool.tensor_scalar(wst2[:, :, :], wst2[:, :, :], SW, 1.0, ALU.mult, ALU.mult).then_inc(wsc_done, 1)
                if G[3]:
                    q, s = G[3]
                    b = 2 * q + s
                    pool.wait_ge(ln2_mv, NI * b + NI)
                    pool.nop(nofuse=True)
                    pool.tensor_scalar(ve2[:, :], mv2[:, :, 1], EPS, 1.0 / (SX * SX), ALU.add, ALU.mult).then_inc(ve2_done, 1)
                    pool.wait_ge(ve2_done, b + 1)
                    wait(pool, xn2_done, NI * b)
                    pool.tensor_tensor(rs2[:, :], ve2[:, :], halfs[:, :], ALU.pow).then_inc(rs2_done, 1)
                if G[0]:
                    q, s = G[0]
                    b = 2 * q + s
                    pool.wait_ge(wsc_done, 2 * b + 2)
                    pool.nop(nofuse=True)
                    pool.tensor_tensor(w1l[:, b, :], wst1[:, :], w1h[:, b, :], ALU.subtract).then_inc(wlo_done, 1)
                    pool.tensor_tensor(w2l[:, bass.ds(b * KC, KC), :], wst2[:, :, :], w2h[:, bass.ds(b * KC, KC), :], ALU.subtract).then_inc(wlo_done, 1)
                if G[4]:
                    q, s = G[4]
                    b = 2 * q + s
                    pool.wait_ge(slot_done, b + 1)
                    pool.wait_ge(lo_done, b + 1)
                    pool.nop(nofuse=True)
                    for k in range(2):
                        for n in range(NI):
                            pool.indirect_dma_start(
                                out=rows_d, out_offset=bass.IndirectOffsetOnAxis(ap=slot[s][:, k * NI + n:k * NI + n + 1], axis=0),
                                in_=rows[s][:, n, :], in_offset=None).then_inc(scattered[s], 16)

            graph_steps(pool, step)

            pool.wait_ge(cnt_ps, 1)
            for s in range(2):
                pool.wait_ge(scattered[s], 16 * 2 * NI * (B // 2))
                pool.wait_ge(x1_out[s], 16 * (B // 2))
            pool.memset(zrow[:, :, :], 0.0).then_inc(zmem, 1)
            pool.iota(s_io[:, :, :], pattern=[[1, NT], [0, E]], base=0, channel_multiplier=0, allow_small_or_imprecise_dtypes=True).then_inc(zmem, 1)

            pool.wait_ge(cw, 1)
            pool.wait_ge(yi_done, 1)

            def gather(g, i):
                for k in range(2):
                    pool.indirect_dma_start(
                        out=gy[i][:, k, :], out_offset=None,
                        in_=y_d, in_offset=bass.IndirectOffsetOnAxis(ap=yi[:, g // NI, k * NI + i:k * NI + i + 1], axis=0)).then_inc(gy_in[i], 16)

            for g in range(NG):
                if g >= NI:
                    pool.wait_ge(c2_done, g - NI + 1)
                gather(g, g % NI)

        @block.tensor
        def _(pe):
            def step(G):
                for t in range(NI):
                    if m := tile_at(G, t, 2):
                        transpose_p(*m)
                    if m := tile_at(G, t, 3):
                        attend(*m)
                    if t == 0 and G[4]:
                        gate(G[4])
                    if t == 1 and G[4]:
                        ranks(G[4])
                    if t == 1 and G[0]:
                        transpose_x(G[0])
                    if t == 2 and G[3]:
                        transpose_x1(G[3])
                    if t == 2 and G[0]:
                        project(G[0], 0)
                    if t == 3 and G[0]:
                        project(G[0], 2)
                        spread_s2(G[0])

            def transpose_x(front):
                q, s = front
                b = 2 * q + s
                pe.wait_ge(xn_done, NI * b + NI)
                for k in range(KC):
                    wait(pe, x2T_sb, KC * (b - 4) + k + 1)
                    for n in range(NI):
                        i_ = pe.transpose(bank[k][:, n * P:(n + 1) * P], xn[:, n, k * P:(k + 1) * P], idf[:, :])
                    i_.then_inc(t1_done, 1)

            def project(front, n0):
                q, s = front
                b = 2 * q + s
                pe.wait_ge(xT_sb, KC * b + KC)
                for n in range(n0, n0 + 2):
                    wait(pe, h_sb, NI * b + n - 1)
                    if n < 2:
                        wait(pe, (lg_done, rk_done)[n], b - 3)
                    for k in range(KC):
                        i_ = pe.matmul(bank[3 + n % 2][:, 0:C + 1], xT[:, k, n * P:(n + 1) * P], wx[:, k, :],
                                       start=(k == 0), stop=(k == KC - 1))
                    i_.then_inc(h_ps, 1)

            def spread_s2(front):
                q, s = front
                b = 2 * q + s
                pe.wait_ge(xT_sb, KC * b + KC)
                wait(pe, a_done, NI * b)
                for k in range(KC):
                    i_ = pe.matmul(bank[2][:, :], wa2r[:, k, :], xT[:, k, :], start=(k == 0), stop=(k == KC - 1))
                i_.then_inc(s2_ps, 1)

            def transpose_p(mid, i):
                q, s = mid
                g = NI * (2 * q + s) + i
                pe.wait_ge(p_done, g + 1)
                wait(pe, pt_sb, g - 1)
                for j in range(NI):
                    i_ = pe.transpose(bank[5 + i % 2][:, j * P:(j + 1) * P], pb[i % 2][:, j * P:(j + 1) * P], idf[:, :])
                i_.then_inc(pt_ps, 1)

            def attend(mid, i):
                q, s = mid
                g = NI * (2 * q + s) + i
                pe.wait_ge(pt_sb, g + 1)
                wait(pe, z_done, g)
                if isinstance(g, int) and g == 0:
                    pe.wait_ge(b1t_sb, 2)
                for j in range(NI):
                    i_ = pe.matmul(bank[7][:, 0:C], pT[i % 2][:, j, :], hs[s][:, j, 0:C],
                                   start=(j == 0), stop=(j == NI - 1))
                i_.then_inc(att_ps, 1)

            def transpose_x1(back):
                q, s = back
                b = 2 * q + s
                pe.wait_ge(xn2_done, NI * b + NI)
                for k in range(KC):
                    pe.wait_ge(xT_sb, min(KC * (b + 3) + k + 1, KC * B) if isinstance(b, int) else KC * (b + 3) + k + 1)
                    for n in range(NI):
                        i_ = pe.transpose(bank[k][:, n * P:(n + 1) * P], xn2[:, n, k * P:(k + 1) * P], idf[:, :])
                    i_.then_inc(t2_done, 1)

            def gate(back):
                q, s = back
                b = 2 * q + s
                pe.wait_ge(x2T_sb, KC * b + KC)
                pe.wait_ge(h_sb, min(NI * (b + 4), NI * B) if isinstance(b, int) else NI * (b + 4))
                for n in range(NI):
                    for k in range(KC):
                        i_ = pe.matmul(gate_ps[:, n * E:(n + 1) * E], x2T[:, k, n * P:(n + 1) * P], wg[:, k, :],
                                       start=(k == 0), stop=(k == KC - 1))
                i_.then_inc(gate_done, 1)

            def ranks(back):
                q, s = back
                b = 2 * q + s
                pe.wait_ge(m_done, b + 1)
                wait(pe, macc_done, b)
                wait(pe, rk_done, b)
                pe.matmul(rank_ps, tri[:, :], m16[:, :, :].rearrange("p n e -> p (n e)"), start=True, stop=False)
                for n in range(NI - 1):
                    pe.matmul(rank_ps[:, (n + 1) * E:].rearrange("p (n e) -> p n e", e=E), ones16[:, :],
                              m16[:, n:n + 1, :].broadcast_to((P, NI - 1 - n, E)), start=False, stop=False)
                pe.matmul(rank_ps.rearrange("p (n e) -> p n e", e=E), ones16[:, :],
                          macc[:, :].unsqueeze(1).broadcast_to((P, NI, E)), start=False, stop=True).then_inc(rank_done, 1)

            pe.wait_ge(consts, 2)
            pe.wait_ge(const_in, 16 * NCONST)
            pe.transpose(bank[7][:, 0:E * MT], xn2[0:E * MT, 0, 0:P], idf[0:E * MT, 0:E * MT]).then_inc(b1t_ps, 1)
            pe.wait_ge(wa_done, 7)
            graph_steps(pe, step)

            pe.wait_ge(macc_done, B)
            pe.matmul(bank[2][:, 0:E], ones16[:, :], macc[:, :], start=True, stop=True).then_inc(cnt_ps, 1)

            def transpose_rows(t, s):
                pe.wait_ge(xs_in[s], 16 * ((t - s) // 2 + 1) if isinstance(t, int) else t * 8 + (16 - 8 * s))
                wait(pe, xst_sb, t - 1)
                for j in range(JT):
                    for h in range(2):
                        for k in range(KC):
                            c = h * KC + k
                            i_ = pe.transpose(bank[s][:, :].bitcast(F16)[:, (c * JT + j) * P:(c * JT + j + 1) * P],
                                              xs[s][:, j, h * C + k * P:h * C + (k + 1) * P], idh[:, :])
                i_.then_inc(xst_ps, 1)

            def hidden(t, s, e):
                pe.wait_ge(xst_sb, t + 1)
                for m in range(FA):
                    wait(pe, act_done, FA * t - FA + m + 1 if not isinstance(t, int) or t > 0 else 0)
                    for half in range(2):
                        o = bank[2 + m][:, half * T:(half + 1) * T]
                        f = (half * FA + m) * P
                        terms = [(w1h, 0, 0), (w1h, 0, 1), (w1l, 0, 0)]
                        n_ = 0
                        for w, _, h in terms:
                            for k in range(KC):
                                i_ = pe.matmul(o, w[:, e * KC + k, f:f + P], xsT[s][:, h * KC + k, :],
                                               start=(n_ == 0), stop=(n_ == 3 * KC - 1))
                                n_ += 1
                    i_.then_inc(ag_ps, 1)

            def results(t, s, e):
                pe.wait_ge(al_done, FA * t + FA)
                wait(pe, y_sb, t - 1)
                for j in range(JT):
                    n_ = 0
                    for k in range(KF):
                        for a, w in ((ah, w2h), (ah, w2l), (al, w2h)):
                            i_ = pe.matmul(bank[6 + s][:, j * C:(j + 1) * C], a[s][:, k, j * P:(j + 1) * P],
                                           w[:, e * KF + k, :], start=(n_ == 0), stop=(n_ == 3 * KF - 1))
                            n_ += 1
                i_.then_inc(y_ps, 1)

            def expert(t):
                return pe.value_load(tabe[0:1, bass.ds(t, 1)], min_val=0, max_val=E - 1)

            pe.wait_ge(table, 2)
            transpose_rows(0, 0)
            hidden(0, 0, expert(0))
            transpose_rows(1, 1)
            hidden(1, 1, expert(1))
            transpose_rows(2, 0)
            results(0, 0, expert(0))
            hidden(2, 0, expert(2))
            transpose_rows(3, 1)
            results(1, 1, expert(1))
            with pe.Fori(1, (NT - 3) // 2) as j:
                hidden(2 * j + 1, 1, expert(2 * j + 1))
                transpose_rows(2 * j + 2, 0)
                results(2 * j, 0, expert(2 * j))
                hidden(2 * j + 2, 0, expert(2 * j + 2))
                transpose_rows(2 * j + 3, 1)
                results(2 * j + 1, 1, expert(2 * j + 1))
            t = NT - 3
            hidden(t + 1, 1, expert(t + 1))
            transpose_rows(t + 2, 0)
            results(t, 0, expert(t))
            hidden(t + 2, 0, expert(t + 2))
            results(t + 1, 1, expert(t + 1))
            results(t + 2, 0, expert(t + 2))

        @block.scalar
        def _(sc):
            act_ = nc.scalar.activation

            def step(G):
                for t in range(NI):
                    if t == 2 and G[0]:
                        q, s = G[0]
                        b = 2 * q + s
                        for k in range(KC):
                            sc.wait_ge(t1_done, KC * b + k + 1)
                            wait(sc, s2_ps, b)
                            act_(xT[:, k, :], bank[k][:, :], ACT.Copy).then_inc(xT_sb, 1)
                    if G[1]:
                        plus_s1(G[1], t)
                    if t == 3 and G[3]:
                        q, s = G[3]
                        b = 2 * q + s
                        for k in range(KC):
                            sc.wait_ge(t2_done, KC * b + k + 1)
                            wait(sc, gate_done, b)
                            act_(x2T[:, k, :], bank[k][:, :], ACT.Copy).then_inc(x2T_sb, 1)
                    if m := tile_at(G, t, 1):
                        probs(*m)
                    if t == 3 and G[2]:
                        q, s = G[2]
                        b = 2 * q + s
                        sc.wait_ge(z_done, NI * b + NI)
                        wait(sc, x1_done, b)
                        act_(ez[:, :, :], zb[s][:, :, :], ACT.Exp, bias=onesf[:, 0:1]).then_inc(ez_done, 1)
                    if m := tile_at(G, t, 2):
                        probs_t(*m)
                    if t == 0 and G[0]:
                        whi(2 * G[0][0] + G[0][1])
                    if t == 2 and G[3]:
                        q, s = G[3]
                        b = 2 * q + s
                        sc.wait_ge(xn2_done, NI * b + NI)
                        wait(sc, scattered[s], 16 * 2 * NI * q)
                        act_(rows[s][:, :, 0:C], xn2[:, :, :], ACT.Copy).then_inc(hi_done, 1)
                    if t >= 2 and G[0]:
                        q, s = G[0]
                        b = 2 * q + s
                        for n in range(2 * t - 4, 2 * t - 2):
                            sc.wait_ge(h_ps, NI * b + n + 1)
                            if n == 0:
                                wait(sc, att_ps, NI * (b - 1))
                                wait(sc, bh_done, b - 1)
                            act_(hs[s][:, n, :], bank[3 + n % 2][:, 0:C + 1], ACT.Copy).then_inc(h_sb, 1)

            def whi(b):
                sc.wait_ge(w_in, 32 * b + 32)
                sc.nop(nofuse=True)
                act_(w1h[:, b, :], wst1[:, :], ACT.Copy, scale=SW).then_inc(whi_done, 1)
                act_(w2h[:, bass.ds(b * KC, KC), :], wst2[:, :, :], ACT.Copy, scale=SW).then_inc(whi_done, 1)

            def plus_s1(mid, i):
                q, s = mid
                b = 2 * q + s
                g = NI * b + i
                sc.wait_ge(s2_ps, b + 1)
                sc.wait_ge(h_sb, NI * b + i + 1)
                wait(sc, em_done, g - 1)
                act_(at_s[i % 2][:, :], bank[2][:, :], ACT.Identity, bias=hs[s][:, i, C:C + 1]).then_inc(a_done, 1)

            def probs(mid, i):
                q, s = mid
                g = NI * (2 * q + s) + i
                sc.wait_ge(nm_done, g + 1)
                wait(sc, ri_done, g - 3)
                wait(sc, pt_ps, g - 1)
                act_(pb[i % 2][:, :], em[i % 2][:, :], ACT.Exp, bias=nmax[:, i % 2, :], accum_out=rsum[:, i, :]).then_inc(p_done, 1)

            def probs_t(mid, i):
                q, s = mid
                g = NI * (2 * q + s) + i
                sc.wait_ge(pt_ps, g + 1)
                wait(sc, att_ps, g - 1)
                act_(pT[i % 2][:, :, :], bank[5 + i % 2][:, :].rearrange("p (j r) -> p j r", j=NI), ACT.Copy).then_inc(pt_sb, 1)

            graph_steps(sc, step)

            sc.wait_ge(table, 2)

            def tile(t, s):
                e = sc.value_load(tabe[0:1, bass.ds(t, 1)], min_val=0, max_val=E - 1)
                for m in range(FA):
                    sc.wait_ge(ag_ps, FA * t + m + 1)
                    wait(sc, act_done, FA * t + m - 1)
                    sc.nop(nofuse=True)
                    act_(sil[m % 2][:, :], bank[2 + m][:, 0:T], ACT.Silu, bias=b1T[:, bass.ds(e * MT + m, 1)],
                         scale=1.0 / (SX * SW)).then_inc(sil_done, 1)
                    if m >= 1:
                        high(t, s, m - 1)
                high(t, s, FA - 1)

            def high(t, s, m):
                sc.wait_ge(act_done, FA * t + m + 1)
                if m == 0:
                    wait(sc, y_ps, t - 1)
                act_(ah[s][:, m, :], act[m % 2][:, :], ACT.Copy, scale=SA / (SX * SW)).then_inc(ah_done, 1)

            tile(0, 0)
            tile(1, 1)
            tile(2, 0)
            with sc.Fori(1, (NT - 1) // 2) as j:
                tile(2 * j + 1, 1)
                tile(2 * j + 2, 0)
            sc.wait_ge(wk_done, 1)
            act_(wk[:, 1, :], dlg_all[:, :, :].rearrange("p b n -> p (b n)"), ACT.Exp).then_inc(ed_done, 1)

        @block.vector
        def _(ve):
            ve.wait_ge(const_in, 16 * NCONST)
            for k in range(KC):
                ve.tensor_tensor_reduce(xn[:, k, :], wx[:, k, 0:C], av[:, 0:C], 1.0, 0.0, ALU.mult, ALU.add, wx[:, k, C:C + 1]).then_inc(wa_done, 1)
                ve.tensor_tensor_reduce(xn[:, 2 + k, :], wx[:, k, 0:C], av[:, C:2 * C], 1.0, 0.0, ALU.mult, ALU.add, wa2[:, k:k + 1]).then_inc(wa_done, 1)
            ve.wait_ge(wa_done, 4)
            ve.wait_ge(onesd, 4)
            for k in range(KC):
                i_ = ve.tensor_scalar(wa2r[:, k, :], onesf[:, :], wa2[:, k:k + 1], None, ALU.mult)
            i_.then_inc(wa_done, 1)
            ve.wait_ge(consts, 2)
            ve.tensor_copy(idh[:, :], idf[:, :])
            ve.tensor_copy(ones16[:, :], onesf[:, :])
            ve.tensor_copy(tri[:, :], trif[:, :]).then_inc(wa_done, 1)
            ve.wait_ge(b1t_ps, 1)
            ve.tensor_copy(b1T[:, :], bank[7][:, 0:E * MT]).then_inc(b1t_sb, 1)
            ve.tensor_scalar(b1S[:, :], bank[7][:, 0:E * MT], SX * SW, None, ALU.mult).then_inc(b1t_sb, 1)
            ve.wait_ge(b1t_sb, 2)
            ve.nop().then_inc(wa_done, 1)

            def step(G):
                for t in range(NI):
                    if m := tile_at(G, t, 4):
                        attended(*m)
                    if t == 0 and G[0]:
                        moments1(*G[0])
                    if t == 1 and G[0]:
                        q, s = G[0]
                        b = 2 * q + s
                        ve.wait_ge(rs1_done, b + 1)
                        wait(ve, t1_done, KC * b)
                        for n in range(NI):
                            ve.tensor_scalar(xn[:, n, :], xt[s][:, n, :], mv1[:, n, 0:1], rs1[:, n:n + 1], ALU.subtract, ALU.mult).then_inc(xn_done, 1)
                    if t == 2 and G[4]:
                        slots(G[4])
                    if t == 3 and G[2]:
                        q, s = G[2]
                        b = 2 * q + s
                        ve.wait_ge(xr_in[s], 16 * q + 16)
                        ve.wait_ge(z_done, NI * b + NI)
                        ve.scalar_tensor_tensor(xr[s][:, :, :], zb[s][:, :, :], -1.0, xr[s][:, :, :], ALU.max, ALU.add).then_inc(rl_done, 1)
                    if G[1]:
                        scores(G[1], t)
                    if t == 3 and G[2]:
                        q, s = G[2]
                        b = 2 * q + s
                        ve.wait_ge(ez_done, b + 1)
                        ve.wait_ge(rl_done, b + 1)
                        ve.scalar_tensor_tensor(xr[s][:, :, :], ez[:, :, :], 1.0, xr[s][:, :, :], ALU.min, ALU.add).then_inc(x1_done, 1)
                    if t == 0 and G[3]:
                        moments2(*G[3])
                    if t == 0 and G[4]:
                        top2(G[4])
                    if t == 1 and G[3]:
                        q, s = G[3]
                        b = 2 * q + s
                        ve.wait_ge(rs2_done, b + 1)
                        wait(ve, t2_done, KC * b)
                        wait(ve, lo_done, b)
                        wait(ve, hi_done, b)
                        for n in range(NI):
                            ve.tensor_scalar(xn2[:, n, :], xr[s][:, n, :], mv2[:, n, 0:1], rs2[:, n:n + 1], ALU.subtract, ALU.mult).then_inc(xn2_done, 1)
                    if t == 2 and G[3]:
                        q, s = G[3]
                        b = 2 * q + s
                        ve.wait_ge(hi_done, b + 1)
                        ve.wait_ge(xn2_done, NI * b + NI)
                        ve.tensor_tensor(rows[s][:, :, C:2 * C], xn2[:, :, :], rows[s][:, :, 0:C], ALU.subtract).then_inc(lo_done, 1)

            def moments1(q, s):
                b = 2 * q + s
                ve.wait_ge(x_in[s], 16 * q + 16)
                wait(ve, rs1_done, b)
                for n in range(NI):
                    ve.bn_stats(st1[:, n, :], xt[s][:, n, :]).then_inc(ln1_st, 1)
                ve.wait_ge(ln1_st, NI * b + NI)
                ve.nop(nofuse=True)
                for n in range(NI):
                    ve.bn_aggr(mv1[:, n, :], st1[:, n, :]).then_inc(ln1_mv, 1)

            def moments2(q, s):
                b = 2 * q + s
                ve.wait_ge(x1_done, b + 1)
                wait(ve, rs2_done, b)
                for n in range(NI):
                    ve.bn_stats(st2[:, n, :], xr[s][:, n, :]).then_inc(ln2_st, 1)
                ve.wait_ge(ln2_st, NI * b + NI)
                ve.nop(nofuse=True)
                for n in range(NI):
                    ve.bn_aggr(mv2[:, n, :], st2[:, n, :]).then_inc(ln2_mv, 1)

            def scores(mid, i):
                q, s = mid
                g = NI * (2 * q + s) + i
                ve.wait_ge(a_done, g + 1)
                ve.scalar_tensor_tensor(at_s[i % 2][:, :], at_s[i % 2][:, :], ALPHA, at_s[i % 2][:, :], ALU.mult, ALU.max).then_inc(lr_done, 1)
                ve.wait_ge(lr_done, g + 1)
                ve.wait_ge(consts, 4)
                wait(ve, p_done, g - 1)
                ve.nop(nofuse=True)
                ve.tensor_tensor_reduce(em[i % 2][:, :], at_s[i % 2][:, :], mask[:, i, :], 1.0, -3.0e38, ALU.mult, ALU.max, rmax[:, i % 2, :]).then_inc(em_done, 1)
                ve.wait_ge(em_done, g + 1)
                ve.tensor_scalar(nmax[:, i % 2, :], rmax[:, i % 2, :], -1.0, None, ALU.mult).then_inc(nm_done, 1)

            def attended(mid, i):
                q, s = mid
                b = 2 * q + s
                g = NI * b + i
                ve.wait_ge(p_done, g + 1)
                wait(ve, z_done, g - 1)
                ve.reciprocal(rinv[:, i % 2, :], rsum[:, i, :]).then_inc(ri_done, 1)
                ve.wait_ge(ri_done, g + 1)
                ve.wait_ge(att_ps, g + 1)
                ve.wait_ge(bh_done, b + 1)
                ve.scalar_tensor_tensor(zb[s][:, i, :], bank[7][:, 0:C], rinv[:, i % 2, :],
                                        zb[s][:, i, :], ALU.mult, ALU.add).then_inc(z_done, 1)

            def top2(back):
                q, s = back
                b = 2 * q + s
                ve.wait_ge(gate_done, b + 1)
                ve.scalar_tensor_tensor(lg[:, :, :], gate_ps.rearrange("p (n e) -> p n e", e=E), 1.0 / SX, bgb[:, :, :], ALU.mult, ALU.add).then_inc(lg_done, 1)
                ve.wait_ge(lg_done, b + 1)
                ve.nop(nofuse=True)
                for n in range(NI):
                    ve.max(mx[:, n, :], lg[:, n, :]).then_inc(mx_done, 1)
                ve.wait_ge(mx_done, NI * b + NI)
                ve.nop(nofuse=True)
                for n in range(NI):
                    ve.max_index(ix[:, n, :], mx[:, n, :], lg[:, n, :]).then_inc(ix_done, 1)
                ve.tensor_tensor(dlg_all[:, b, :], mx[:, :, 1], mx[:, :, 0], ALU.subtract)
                ve.wait_ge(ix_done, NI * b + NI)
                ve.tensor_copy(ixf[:, :, :], ix[:, :, 0:2].rearrange("p n k -> p k n")).then_inc(ixf_done, 1)
                ve.wait_ge(ixf_done, b + 1)
                ve.tensor_tensor(oh[:, :, :], iota2[:, :, :], ixf[:, :, :].rearrange("p k n -> p (k n)").unsqueeze(2).broadcast_to((P, 2 * NI, E)), ALU.is_equal).then_inc(oh_done, 1)
                ve.wait_ge(oh_done, b + 1)
                wait(ve, rank_done, b)
                ve.tensor_tensor(m16[:, :, :], oh[:, 0:NI, :], oh[:, NI:2 * NI, :], ALU.add).then_inc(m_done, 1)

            def slots(back):
                q, s = back
                b = 2 * q + s
                ve.wait_ge(m_done, b + 1)
                ve.tensor_reduce(msum[:, :], m16[:, :, :].rearrange("p n e -> p e n"), AX, ALU.add).then_inc(msum_done, 1)
                ve.wait_ge(rank_done, b + 1)
                for k in range(2):
                    i_ = ve.tensor_tensor(rk[:, k * NI:(k + 1) * NI, :], oh[:, k * NI:(k + 1) * NI, :],
                                          rank_ps.rearrange("p (n e) -> p n e", e=E), ALU.mult)
                i_.then_inc(rk_done, 1)
                ve.wait_ge(msum_done, b + 1)
                ve.tensor_tensor(macc[:, :], macc[:, :], msum[:, :], ALU.add).then_inc(macc_done, 1)
                ve.wait_ge(rk_done, b + 1)
                ve.tensor_reduce(rkr[:, :], rk[:, :, :], AX, ALU.add).then_inc(rkr_done, 1)
                ve.wait_ge(rkr_done, b + 1)
                wait(ve, scattered[s], 16 * 2 * NI * q)
                ve.scalar_tensor_tensor(slot[s][:, :], ixf[:, :, :].rearrange("p k n -> p (k n)"), float(R), rkr[:, :], ALU.mult, ALU.add).then_inc(slot_done, 1)
                ve.tensor_copy(rank_all[:, b, :], rkr[:, :])
                ve.tensor_copy(exp_all[:, b, :], ixf[:, :, :].rearrange("p k n -> p (k n)"))

            graph_steps(ve, step)

            n_ = 0

            def then(i_):
                nonlocal n_
                i_.then_inc(tb, 1)
                n_ += 1
                ve.wait_ge(tb, n_)

            ve.wait_ge(cnt_ps, 1)
            ve.wait_ge(zmem, 2)
            then(ve.tensor_copy(cnt[:, :], bank[2][:, 0:E]))
            ve.tensor_copy(cnti[:, :], cnt[:, :])
            ve.memset(one8[:, :], 1.0)
            then(ve.tensor_scalar(cntp[:, :], cnt[:, :], float(T - 1), None, ALU.add))
            then(ve.tensor_scalar(nti[:, :], cntp[:, :], T.bit_length() - 1, None, ALU.logical_shift_right))
            then(ve.tensor_copy(ntf[:, :], nti[:, :]))
            then(ve.tensor_tensor_scan(ends[:, :], one8[:, :], ntf[:, :], 0.0, ALU.mult, ALU.add))
            then(ve.tensor_tensor(base[:, :], ends[:, :], ntf[:, :], ALU.subtract))
            then(ve.tensor_scalar(base[:, :], base[:, :], float(T), None, ALU.mult))
            then(ve.tensor_tensor(ge[:, :, :], s_io[:, :, :], ends[0:1, :].unsqueeze(1).broadcast_to((1, NT, E)), ALU.is_ge))
            ve.tensor_reduce(ex[:, :], ge[:, :, :], AX, ALU.add)
            then(ve.tensor_tensor(gn[:, :, :], ge[:, :, :], ntf[0:1, :].unsqueeze(1).broadcast_to((1, NT, E)), ALU.mult))
            then(ve.tensor_reduce(stt[:, :], gn[:, :, :], AX, ALU.add))
            ve.tensor_scalar(tabe[:, :], ex[:, :], float(E - 1), None, ALU.min)
            then(ve.tensor_tensor(srow[:, :], s_io[:, :, 0], stt[:, :], ALU.subtract))
            then(ve.tensor_scalar(srow[:, :], srow[:, :], float(T), None, ALU.mult))
            then(ve.scalar_tensor_tensor(srow[:, :], ex[:, :], float(R), srow[:, :], ALU.mult, ALU.add))
            then(ve.tensor_scalar(tabr[:, :], srow[:, :], float(E * R), None, ALU.min))
            ve.nop().then_inc(table, 2)
            then(ve.tensor_copy(yf[:, :, :], rank_all[:, :, :]))
            for e in range(E):
                then(ve.tensor_scalar(ybs[:, :, :], exp_all[:, :, :], float(e), base[:, e:e + 1], ALU.is_equal, ALU.mult))
                then(ve.tensor_tensor(yf[:, :, :], yf[:, :, :], ybs[:, :, :], ALU.add))
            ve.tensor_copy(yi[:, :, :], yf[:, :, :]).then_inc(yi_done, 1)

            def rows_t(t, s):
                ve.wait_ge(xst_ps, t + 1)
                wait(ve, ag_ps, FA * (t - 1))
                ve.tensor_copy(xsT[s][:, :, :].rearrange("p c r -> p (c r)"), bank[s][:, :].bitcast(F16)).then_inc(xst_sb, 1)

            def tile(t, s, more=True):
                e = ve.value_load(tabe[0:1, bass.ds(t, 1)], min_val=0, max_val=E - 1)
                for m in range(FA):
                    ve.wait_ge(sil_done, FA * t + m + 1)
                    wait(ve, ah_done, FA * t + m - 1)
                    wait(ve, al_done, FA * t + m - 1)
                    ve.scalar_tensor_tensor(act[m % 2][:, :], bank[2 + m][:, T:2 * T], b1S[:, bass.ds(e * MT + FA + m, 1)],
                                            sil[m % 2][:, :], ALU.add, ALU.mult).then_inc(act_done, 1)
                    if m >= 1:
                        low(t, s, m - 1)
                    if m == 1 and more:
                        rows_t(t + 1, 1 - s)
                low(t, s, FA - 1)

            def low(t, s, m):
                ve.wait_ge(ah_done, FA * t + m + 1)
                ve.wait_ge(act_done, FA * t + m + 1)
                ve.scalar_tensor_tensor(al[s][:, m, :], act[m % 2][:, :], SA / (SX * SW), ah[s][:, m, :], ALU.mult, ALU.subtract).then_inc(al_done, 1)

            def result(t, s):
                e = ve.value_load(tabe[0:1, bass.ds(t, 1)], min_val=0, max_val=E - 1)
                ve.wait_ge(y_ps, t + 1)
                q = (t - s) // 2 if isinstance(t, int) else None
                if q is None or q > 0:
                    ve.wait_ge(y_out[s], 16 * q if q is not None else t * 8 - 8 * s)
                ve.scalar_tensor_tensor(ys[s][:, :, :], bank[6 + s][:, :].rearrange("p (j c) -> p j c", j=JT), 1.0 / (SA * SW),
                                        b2b[:, bass.ds(e, 1), :].broadcast_to((P, JT, C)), ALU.mult, ALU.add).then_inc(y_sb, 1)

            rows_t(0, 0)
            tile(0, 0)
            tile(1, 1)
            result(0, 0)
            tile(2, 0)
            result(1, 1)
            tile(3, 1)
            result(2, 0)
            with ve.Fori(2, (NT - 1) // 2) as j:
                tile(2 * j, 0)
                result(2 * j - 1, 1)
                tile(2 * j + 1, 1)
                result(2 * j, 0)
            tile(NT - 1, 0, more=False)
            result(NT - 2, 1)
            result(NT - 1, 0)

            ve.nop().then_inc(wk_done, 1)
            ve.wait_ge(ed_done, 1)
            then(ve.tensor_scalar(wk[:, 0, :], wk[:, 1, :], 1.0, None, ALU.add))
            then(ve.reciprocal(wk[:, 0, :], wk[:, 0, :]))
            then(ve.tensor_tensor(wk[:, 1, :], wk[:, 0, :], wk[:, 1, :], ALU.mult))
            for g in range(NG):
                i, s = g % NI, (g // NI) % 2
                if i == 0:
                    ve.wait_ge(xo_in[s], 16 * (g // NI // 2 + 1))
                ve.wait_ge(gy_in[i], 32 * (g // NI + 1))
                ve.scalar_tensor_tensor(xo[s][:, i, :], gy[i][:, 0, :], wk[:, 0, g:g + 1], xo[s][:, i, :], ALU.mult, ALU.add).then_inc(c1_done, 1)
                ve.wait_ge(c1_done, g + 1)
                ve.scalar_tensor_tensor(xo[s][:, i, :], gy[i][:, 1, :], wk[:, 1, g:g + 1], xo[s][:, i, :], ALU.mult, ALU.add).then_inc(c2_done, 1)


_INS = ['x', 'adj', 'L0_gnn_W', 'L0_gnn_a', 'L0_gnn_beta', 'L0_ffn_Wg', 'L0_ffn_bg', 'L0_ffn_W1', 'L0_ffn_b1', 'L0_ffn_W2', 'L0_ffn_b2']
_OUTS = [((16, 512, 256), 'float32')]


def kernel(**inputs):
    import numpy as _np
    import concourse.bacc as _bacc
    from concourse import mybir as _mybir
    from concourse.bass_utils import run_bass_kernel_spmd as _run

    nc = _bacc.Bacc("TRN2", target_bir_lowering=False, num_devices=1)
    arrays, args = {}, []
    for name in _INS:
        a = _np.ascontiguousarray(inputs[name])
        arrays[f"in_{name}_dram"] = a
        args.append(nc.dram_tensor(f"in_{name}_dram", a.shape, _mybir.dt.from_np(a.dtype), kind="ExternalInput").ap())
    for i, (shape, dtype) in enumerate(_OUTS):
        dt = _mybir.dt.from_np(_np.dtype(dtype))
        args.append(nc.dram_tensor(f"out_{i}_dram", shape, dt, kind="ExternalOutput").ap())
    build_gat_moe(nc, *args)
    r = _run(nc, [arrays], core_ids=[0])
    return r.results[0]["out_0_dram"]
```

```python
from contextlib import ExitStack

import concourse.bass as bass
from concourse import mybir

F32 = mybir.dt.float32
F16 = mybir.dt.float16
I16 = mybir.dt.int16
BF16 = mybir.dt.bfloat16
I32 = mybir.dt.int32
U32 = mybir.dt.uint32
ALU = mybir.AluOpType
ACT = mybir.ActivationFunctionType
AX = mybir.AxisListType.X

P = 128
T = 256
JT = T // P
SX = 16.0
SW = 64.0
SA = 16.0
EPS = 1e-5
ALPHA = 0.2


def put(value, least=1):
    return not isinstance(value, int) or value >= least


def wait(eng, semaphore, value):
    if put(value):
        eng.wait_ge(semaphore, value)


def build_gat_moe(nc, x, adj, gW, ga, gbeta, Wg, bg, W1, b1, W2, b2, out):
    B, N, C = x.shape
    NI = N // P
    KC = C // P
    E = Wg.shape[1]
    DFF = W2.shape[1]
    FA = DFF // P
    H1 = 2 * DFF
    MT = H1 // P
    KF = DFF // P
    TOK = B * N
    NG = B * NI
    NT = 2 * TOK // T + E - 1
    R = TOK + T
    NCH = E * KC
    assert NCH == B and KC == 2 and KF == 2 * KC and NT % 2 == 1

    x_v = x.rearrange("b (p n) c -> b p n c", n=NI)
    adj_v = adj.rearrange("(p n) j -> p n j", n=NI)
    W1_v = W1.rearrange("e (k p) f -> (e k) p f", p=P)
    W2_v = W2.rearrange("e (a k p) c -> (e a) p k c", p=P, k=KC)

    RW = 2 * C + 8
    TOKEN, ED, E0 = 0, 1, 2
    rows_d = nc.dram_tensor("expert_rows", (E * R + T, RW), I16, kind="Internal").ap()
    acc_d = nc.dram_tensor("sums", (TOK + T, C), F32, kind="Internal").ap()
    x1_v = acc_d[0:TOK, :].rearrange("(b p n) c -> b p n c", p=P, n=NI)

    def tile_of(rows):
        return rows.rearrange("(p j) c -> p j c", j=JT)

    def meta(t, k, dt=F32):
        return t[:, :, 2 * C + 2 * k:2 * C + 2 * k + 2].bitcast(dt)[:, :, 0]

    at = [(nc.sbuf_base + 31) // 32 * 32]

    def sb(name, shape, dt):
        size = mybir.dt.size(dt)
        for d in shape[1:]:
            size *= d
        t = nc.alloc_sbuf_tensor_at(name, list(shape), dt, offset=at[0])
        at[0] += (size + 31) // 32 * 32
        assert at[0] <= nc.sbuf_usable_end, (name, at[0])
        return t

    w1h = sb("w1h", [P, E * KC, H1], F16)
    w1l = sb("w1l", [P, E * KC, H1], F16)
    w2h = sb("w2h", [P, E * KF, C], F16)
    w2l = sb("w2l", [P, E * KF, C], F16)
    b1T = sb("b1T", [P, E * MT], F32)
    b1S = sb("b1S", [P, E * MT], F32)
    b2b = sb("b2b", [P, E, C], F32)
    pad = sb("pad", [P, JT, RW], I16)
    s_io = sb("s_io", [P, NT], F32)
    macc = sb("macc", [P, E], BF16)
    ones16 = sb("ones16", [P, P], BF16)
    idh = sb("idh", [P, P], F16)
    phase = at[0]

    wst1 = sb("wst1", [P, H1], F32)
    wst2 = sb("wst2", [P, KC, C], F32)
    xt = [sb(f"xt{i}", [P, NI, C], F32) for i in range(2)]
    xn = sb("xn", [P, NI, C], F32)
    xT = sb("xT", [P, KC, N], F32)
    tokc = [sb(f"tokc{i}", [P, NI], F32) for i in range(2)]
    idf = sb("idf", [P, P], F32)
    onesf = sb("onesf", [P, P], F32)
    tri = sb("tri", [P, P], BF16)
    trif = sb("trif", [P, P], F32)
    wx = sb("wx", [P, KC, C + 1], F32)
    av = sb("av", [P, 2 * C], F32)
    wa2 = sb("wa2", [P, KC], F32)
    wa2r = sb("wa2r", [P, KC, P], F32)
    betat = sb("betat", [P, 1], F32)
    bgb = sb("bgb", [P, NI, E], F32)
    wg = sb("wg", [P, KC, E], F32)
    iota2 = sb("iota2", [P, 2 * NI, E], F32)
    halfs = sb("halfs", [P, NI], F32)
    mask = sb("mask", [P, NI, N], F32)
    xr = [sb(f"xr{i}", [P, NI, C], F32) for i in range(2)]
    xn2 = sb("xn2", [P, NI, C], F32)
    x2T = sb("x2T", [P, KC, N], F32)
    hs = [sb(f"hs{i}", [P, NI, C + 1], F32) for i in range(2)]
    zb = [sb(f"zb{i}", [P, NI, C], F32) for i in range(2)]
    ez = sb("ez", [P, NI, C], F32)
    at_s = [sb(f"at_s{i}", [P, N], F32) for i in range(2)]
    em = [sb(f"em{i}", [P, N], F32) for i in range(2)]
    pb = [sb(f"pb{i}", [P, N], F32) for i in range(2)]
    pT = [sb(f"pT{i}", [P, NI, P], F32) for i in range(2)]
    rows = [sb(f"rows{i}", [P, NI, RW], I16) for i in range(2)]
    st1 = sb("st1", [P, NI, 6], F32)
    mv1 = sb("mv1", [P, NI, 2], F32)
    st2 = sb("st2", [P, NI, 6], F32)
    mv2 = sb("mv2", [P, NI, 2], F32)
    ve1 = sb("ve1", [P, NI], F32)
    ve2 = sb("ve2", [P, NI], F32)
    rs1 = sb("rs1", [P, NI], F32)
    rs2 = sb("rs2", [P, NI], F32)
    rmax = sb("rmax", [P, 2, 1], F32)
    nmax = sb("nmax", [P, 2, 1], F32)
    rsum = sb("rsum", [P, 4, 1], F32)
    rinv = sb("rinv", [P, 2, 1], F32)
    lg = sb("lg", [P, NI, E], F32)
    mx = sb("mx", [P, NI, E], F32)
    ix = sb("ix", [P, NI, E], U32)
    ixf = sb("ixf", [P, 2, NI], F32)
    oh = sb("oh", [P, 2 * NI, E], F32)
    m16 = sb("m16", [P, NI, E], BF16)
    msum = sb("msum", [P, E], F32)
    rk = sb("rk", [P, 2 * NI, E], F32)
    rkr = sb("rkr", [P, 2 * NI], F32)
    slot = [sb(f"slot{i}", [P, 2 * NI], I32) for i in range(2)]

    at[0] = phase
    cnt = sb("cnt", [P, E], F32)
    cnti = sb("cnti", [P, E], I32)
    cntp = sb("cntp", [P, E], I32)
    nti = sb("nti", [P, E], I32)
    ntf = sb("ntf", [P, E], F32)
    one8 = sb("one8", [P, E], F32)
    ends = sb("ends", [P, E], F32)
    ge = sb("ge", [P, NT, E], F32)
    gn = sb("gn", [P, NT, E], F32)
    ex = sb("ex", [P, NT], F32)
    stt = sb("stt", [P, NT], F32)
    srow = sb("srow", [P, NT], F32)
    tabe = sb("tabe", [P, NT], I32)
    tabr = sb("tabr", [P, NT], I32)
    xs = [sb(f"xs{i}", [P, JT, RW], I16) for i in range(2)]
    xsT = [sb(f"xsT{i}", [P, 2 * KC, T], F16) for i in range(2)]
    sil = [sb(f"sil{i}", [P, T], F32) for i in range(2)]
    act = [sb(f"act{i}", [P, T], F32) for i in range(2)]
    ah = [sb(f"ah{i}", [P, KF, T], F16) for i in range(2)]
    al = [sb(f"al{i}", [P, KF, T], F16) for i in range(2)]
    ys = [sb(f"ys{i}", [P, JT, C], F32) for i in range(2)]
    tok = [sb(f"tok{i}", [P, JT], I32) for i in range(2)]
    wden = sb("wden", [P, JT], F32)
    wsel = sb("wsel", [P, JT], F32)
    winv = sb("winv", [P, JT], F32)
    wrow = [sb(f"wrow{i}", [P, JT], F32) for i in range(2)]

    with ExitStack() as ctx:
        bank = [ctx.enter_context(nc.psum_tensor(f"bank{i}", [P, 512], F32)) for i in range(8)]
        gate_ps = bank[3][:, 0:NI * E]
        rank_ps = bank[4][:, 0:NI * E]

        def sem(name):
            return ctx.enter_context(nc.semaphore(name))

        const_in = sem("const_in")
        x_in = [sem(f"x_in{i}") for i in range(2)]
        xr_in = [sem(f"xr_in{i}") for i in range(2)]
        w_in = sem("w_in")
        adj_in = sem("adj_in")
        x1_out = [sem(f"x1_out{i}") for i in range(2)]
        scattered = [sem(f"scattered{i}") for i in range(2)]
        consts = sem("consts")
        onesd = sem("onesd")
        wa_done = sem("wa_done")
        b1t_ps = sem("b1t_ps")
        b1t_sb = sem("b1t_sb")
        ln1_st = sem("ln1_st")
        ln1_mv = sem("ln1_mv")
        ve1_done = sem("ve1_done")
        rs1_done = sem("rs1_done")
        xn_done = sem("xn_done")
        t1_done = sem("t1_done")
        xT_sb = sem("xT_sb")
        h_ps = sem("h_ps")
        h_sb = sem("h_sb")
        s2_ps = sem("s2_ps")
        bh_done = sem("bh_done")
        a_done = sem("a_done")
        lr_done = sem("lr_done")
        em_done = sem("em_done")
        nm_done = sem("nm_done")
        p_done = sem("p_done")
        pt_ps = sem("pt_ps")
        pt_sb = sem("pt_sb")
        att_ps = sem("att_ps")
        ri_done = sem("ri_done")
        z_done = sem("z_done")
        ez_done = sem("ez_done")
        rl_done = sem("rl_done")
        x1_done = sem("x1_done")
        ln2_st = sem("ln2_st")
        ln2_mv = sem("ln2_mv")
        ve2_done = sem("ve2_done")
        rs2_done = sem("rs2_done")
        xn2_done = sem("xn2_done")
        hi_done = sem("hi_done")
        lo_done = sem("lo_done")
        t2_done = sem("t2_done")
        x2T_sb = sem("x2T_sb")
        gate_done = sem("gate_done")
        lg_done = sem("lg_done")
        mx_done = sem("mx_done")
        ix_done = sem("ix_done")
        ixf_done = sem("ixf_done")
        oh_done = sem("oh_done")
        m_done = sem("m_done")
        rank_done = sem("rank_done")
        msum_done = sem("msum_done")
        macc_done = sem("macc_done")
        rk_done = sem("rk_done")
        rkr_done = sem("rkr_done")
        slot_done = sem("slot_done")
        d_done = sem("d_done")
        ed_done = sem("ed_done")
        whi_done = sem("whi_done")
        wsc_done = sem("wsc_done")
        wlo_done = sem("wlo_done")
        cnt_ps = sem("cnt_ps")
        tb = sem("tb")
        table = sem("table")
        zdone = sem("zdone")
        padc = sem("padc")
        xs_in = [sem(f"xs_in{i}") for i in range(2)]
        xst_ps = sem("xst_ps")
        xst_sb = sem("xst_sb")
        ag_ps = sem("ag_ps")
        sil_done = sem("sil_done")
        act_done = sem("act_done")
        ah_done = sem("ah_done")
        al_done = sem("al_done")
        y_ps = sem("y_ps")
        y_sb = sem("y_sb")
        wm = sem("wm")
        wrow_done = sem("wrow_done")
        yb_done = sem("yb_done")
        added = [sem(f"added{i}") for i in range(2)]
        fin_out = sem("fin_out")

        NCONST = 10
        block = ctx.enter_context(nc.Block())

        LAGS = 5
        LAST = B + LAGS - 1

        def graph_steps(eng, step, tail=0):
            def one(i):
                step([((i - lag) // 2, (i - lag) % 2) if 0 <= i - lag < B else None for lag in range(LAGS)])
            for i in range(6):
                one(i)
            with eng.Fori(3, (B - tail) // 2) as j:
                for u in range(2):
                    step([(j + (u - lag) // 2, (u - lag) % 2) for lag in range(LAGS)])
            for i in range(B - tail, LAST):
                one(i)

        def tile_at(G, t, lag):
            g = G[1] if t >= lag else G[2]
            return g and (g, (t - lag) % NI)

        @block.sync
        def _(sp):
            sp.dma_start(xt[0][:, :, :], x_v[0]).then_inc(x_in[0], 16)
            sp.dma_start(wx[:, :, 0:C], gW.rearrange("(k p) f -> p k f", p=P)).then_inc(const_in, 16)
            sp.dma_start(av[:, :], ga.rearrange("f o -> (f o)").partition_broadcast(P)).then_inc(const_in, 16)
            sp.dma_start(betat[:, :], gbeta.partition_broadcast(P)).then_inc(const_in, 16)
            sp.dma_start(wg[:, :, :], Wg.rearrange("(k p) e -> p k e", p=P)).then_inc(const_in, 16)
            for n in range(NI):
                sp.dma_start(bgb[:, n, :], bg.partition_broadcast(P)).then_inc(const_in, 16)
            adj_nat = [xr[i][:, :, :].rearrange("p n c -> p (n c)").rearrange("p (n j) -> p n j", j=N) for i in range(2)]
            for i in range(2):
                sp.dma_start(adj_nat[i], adj_v[:, 2 * i:2 * i + 2, :]).then_inc(adj_in, 16)
            sp.dma_start(xn2[0:E * MT, 0, 0:P], b1.rearrange("e (m p) -> (e m) p", p=P)).then_inc(const_in, 16)
            sp.dma_start(b2b[:, :, :], b2.rearrange("e c -> (e c)").partition_broadcast(P)).then_inc(const_in, 16)

            sp.wait_ge(padc, 3)
            sp.dma_start(tile_of(rows_d[E * R:E * R + T, :]), pad[:, :, :]).then_inc(zdone, 16)
            sp.dma_start(tile_of(acc_d[TOK:TOK + T, :]), pad[:, :, 0:2 * C].bitcast(F32)).then_inc(zdone, 16)

            def step(G):
                if G[0]:
                    q, s = G[0]
                    b = 2 * q + s
                    if not isinstance(b, int) or b + 1 < B:
                        wait(sp, xn_done, NI * b)
                        sp.dma_start(xt[1 - s][:, :, :], x_v[b + 1]).then_inc(x_in[1 - s], 16)
                    wait(sp, wlo_done, 2 * b)
                    sp.dma_start(wst1[:, :], W1_v[b]).then_inc(w_in, 16)
                    sp.dma_start(wst2[:, :, :], W2_v[b]).then_inc(w_in, 16)
                if G[1]:
                    q, s = G[1]
                    b = 2 * q + s
                    if put(q):
                        sp.wait_ge(x1_out[s], 16 * q)
                        sp.wait_ge(xn2_done, (b - 1) * NI)
                    else:
                        sp.wait_ge(consts, 4)
                    sp.dma_start(xr[s][:, :, :], x_v[b]).then_inc(xr_in[s], 16)
                if G[2]:
                    q, s = G[2]
                    b = 2 * q + s
                    sp.wait_ge(x1_done, b + 1)
                    sp.dma_start(x1_v[b], xr[s][:, :, :]).then_inc(x1_out[s], 16)

            graph_steps(sp, step, tail=2)

            sp.wait_ge(table, 1)
            for e in range(E):
                c_e = sp.value_load(cnti[0:1, e:e + 1], min_val=0, max_val=TOK)
                sp.dma_start(tile_of(rows_d[bass.ds(c_e + e * R, T), :]), pad[:, :, :]).then_inc(zdone, 16)
            sp.wait_ge(zdone, 16 * (E + 2))
            for s in range(2):
                sp.wait_ge(scattered[s], 16 * 2 * NI * (B // 2))
                sp.wait_ge(x1_out[s], 16 * (B // 2))

            def load_rows(t, s):
                r = sp.value_load(tabr[0:1, bass.ds(t, 1)], min_val=0, max_val=E * R)
                sp.dma_start(xs[s][:, :, :], tile_of(rows_d[bass.ds(r, T), :])).then_inc(xs_in[s], 16)

            sp.wait_ge(table, 3)
            load_rows(0, 0)
            load_rows(1, 1)
            with sp.Fori(0, (NT - 3) // 2) as j:
                for s in range(2):
                    sp.wait_ge(xst_ps, 2 * j + s + 1)
                    sp.wait_ge(wrow_done, 2 * j + s + 1)
                    load_rows(2 * j + s + 2, s)
            sp.wait_ge(xst_ps, NT - 2)
            sp.wait_ge(wrow_done, NT - 2)
            load_rows(NT - 1, 0)
            sp.wait_ge(added[0], 16 * JT * ((NT + 1) // 2))
            sp.wait_ge(added[1], 16 * JT * (NT // 2))
            out_f = out.rearrange("b n c -> (b n) c")
            for i in range(4):
                part = slice(i * TOK // 4, (i + 1) * TOK // 4)
                sp.dma_start(out_f[part, :].rearrange("(a r) c -> a (r c)", a=16), acc_d[part, :].rearrange("(a r) c -> a (r c)", a=16)).then_inc(fin_out, 16)
            sp.wait_ge(fin_out, 64)

        @block.gpsimd
        def _(pool):
            pool.memset(onesf[:, :], 1.0).then_inc(onesd, 1)
            pool.memset(halfs[:, :], -0.5).then_inc(onesd, 1)
            pool.memset(macc[:, :], 0.0).then_inc(onesd, 1)
            pool.iota(iota2[:, :, :], pattern=[[0, 2 * NI], [1, E]], base=0, channel_multiplier=0, allow_small_or_imprecise_dtypes=True).then_inc(onesd, 1)
            for s in range(2):
                pool.iota(tokc[s][:, :], pattern=[[1, NI]], base=s * N, channel_multiplier=NI, allow_small_or_imprecise_dtypes=True)
            pool.iota(s_io[:, :], pattern=[[1, NT]], base=0, channel_multiplier=0, allow_small_or_imprecise_dtypes=True).then_inc(onesd, 1)
            for s in range(2):
                pool.memset(rows[s][:, :, 2 * C:RW], 0)
            pool.memset(pad[:, :, :], 0).then_inc(padc, 1)
            pool.wait_ge(padc, 1)
            pool.iota(meta(pad, TOKEN, I32), pattern=[[1, JT]], base=TOK, channel_multiplier=JT).then_inc(padc, 2)
            pool.wait_ge(onesd, 5)
            pool.affine_select(idf[:, :], onesf[:, :], pattern=[[-1, P]], compare_op=ALU.is_equal, fill=0.0, base=0, channel_multiplier=1).then_inc(consts, 1)
            pool.affine_select(trif[:, :], onesf[:, :], pattern=[[1, P]], compare_op=ALU.is_gt, fill=0.0, base=0, channel_multiplier=-1).then_inc(consts, 1)
            adj_nat = [xr[i][:, :, :].rearrange("p n c -> p (n c)").rearrange("p (n j) -> p n j", j=N) for i in range(2)]
            pool.wait_ge(adj_in, 32)
            for n in range(NI):
                src = adj_nat[n // 2][:, n % 2, :].rearrange("p (q m) -> p m q", m=NI)
                i_ = pool.tensor_scalar(mask[:, n, :].rearrange("p (m q) -> p m q", m=NI), src, 1.0, 1.0, ALU.mult, ALU.mult)
                if n % 2:
                    i_.then_inc(consts, 1)
            pool.wait_ge(const_in, 16 * NCONST)

            def step(G):
                if G[1]:
                    q, s = G[1]
                    b = 2 * q + s
                    pool.wait_ge(h_sb, NI * b + NI)
                    wait(pool, rl_done, b - 1)
                    wait(pool, ez_done, b - 1)
                    pool.nop(nofuse=True)
                    pool.tensor_scalar(zb[s][:, :, :], hs[s][:, :, 0:C], betat[:, 0:1], -1.0, ALU.mult, ALU.add).then_inc(bh_done, 1)
                if G[0]:
                    q, s = G[0]
                    b = 2 * q + s
                    pool.wait_ge(ln1_mv, NI * b + NI)
                    pool.nop(nofuse=True)
                    pool.tensor_scalar(ve1[:, :], mv1[:, :, 1], 1.0, EPS, ALU.mult, ALU.add).then_inc(ve1_done, 1)
                    pool.wait_ge(ve1_done, b + 1)
                    wait(pool, xn_done, NI * b)
                    pool.tensor_tensor(rs1[:, :], ve1[:, :], halfs[:, :], ALU.pow).then_inc(rs1_done, 1)
                if G[0]:
                    q, s = G[0]
                    b = 2 * q + s
                    pool.wait_ge(whi_done, 2 * b + 2)
                    pool.nop(nofuse=True)
                    pool.tensor_scalar(wst1[:, :], wst1[:, :], SW, 1.0, ALU.mult, ALU.mult).then_inc(wsc_done, 1)
                    pool.tensor_scalar(wst2[:, :, :], wst2[:, :, :], SW, 1.0, ALU.mult, ALU.mult).then_inc(wsc_done, 1)
                if G[3]:
                    q, s = G[3]
                    b = 2 * q + s
                    pool.wait_ge(ln2_mv, NI * b + NI)
                    pool.nop(nofuse=True)
                    pool.tensor_scalar(ve2[:, :], mv2[:, :, 1], EPS, 1.0 / (SX * SX), ALU.add, ALU.mult).then_inc(ve2_done, 1)
                    pool.wait_ge(ve2_done, b + 1)
                    wait(pool, xn2_done, NI * b)
                    pool.tensor_tensor(rs2[:, :], ve2[:, :], halfs[:, :], ALU.pow).then_inc(rs2_done, 1)
                if G[0]:
                    q, s = G[0]
                    b = 2 * q + s
                    pool.wait_ge(wsc_done, 2 * b + 2)
                    pool.nop(nofuse=True)
                    pool.tensor_tensor(w1l[:, b, :], wst1[:, :], w1h[:, b, :], ALU.subtract).then_inc(wlo_done, 1)
                    pool.tensor_tensor(w2l[:, bass.ds(b * KC, KC), :], wst2[:, :, :], w2h[:, bass.ds(b * KC, KC), :], ALU.subtract).then_inc(wlo_done, 1)
                if G[4]:
                    q, s = G[4]
                    b = 2 * q + s
                    pool.wait_ge(slot_done, b + 1)
                    pool.wait_ge(lo_done, b + 1)
                    pool.wait_ge(ed_done, b + 1)
                    pool.nop(nofuse=True)
                    for k in range(2):
                        for n in range(NI):
                            pool.indirect_dma_start(
                                out=rows_d, out_offset=bass.IndirectOffsetOnAxis(ap=slot[s][:, k * NI + n:k * NI + n + 1], axis=0),
                                in_=rows[s][:, n, :], in_offset=None).then_inc(scattered[s], 16)

            graph_steps(pool, step)

            def add(t, s, before):
                pool.wait_ge(y_sb, t + 1)
                wait(pool, added[1 - s], 16 * JT * before)
                pool.nop(nofuse=True)
                for j in range(JT):
                    pool.indirect_dma_start(
                        out=acc_d, out_offset=bass.IndirectOffsetOnAxis(ap=tok[s][:, j:j + 1], axis=0),
                        in_=ys[s][:, j, :], in_offset=None, compute_op=ALU.add).then_inc(added[s], 16)

            for s in range(2):
                pool.wait_ge(x1_out[s], 16 * (B // 2))
            add(0, 0, 0)
            add(1, 1, 1)
            with pool.Fori(1, (NT - 1) // 2) as j:
                add(2 * j, 0, j)
                add(2 * j + 1, 1, j + 1)
            add(NT - 1, 0, NT // 2)

        @block.tensor
        def _(pe):
            def step(G):
                for t in range(NI):
                    if m := tile_at(G, t, 2):
                        transpose_p(*m)
                    if m := tile_at(G, t, 3):
                        attend(*m)
                    if t == 0 and G[4]:
                        gate(G[4])
                    if t == 1 and G[4]:
                        ranks(G[4])
                    if t == 1 and G[0]:
                        transpose_x(G[0])
                    if t == 2 and G[3]:
                        transpose_x1(G[3])
                    if t == 2 and G[0]:
                        project(G[0], 0)
                    if t == 3 and G[0]:
                        project(G[0], 2)
                        spread_s2(G[0])

            def transpose_x(front):
                q, s = front
                b = 2 * q + s
                pe.wait_ge(xn_done, NI * b + NI)
                for k in range(KC):
                    wait(pe, x2T_sb, KC * (b - 4) + k + 1)
                    for n in range(NI):
                        i_ = pe.transpose(bank[k][:, n * P:(n + 1) * P], xn[:, n, k * P:(k + 1) * P], idf[:, :])
                    i_.then_inc(t1_done, 1)

            def project(front, n0):
                q, s = front
                b = 2 * q + s
                pe.wait_ge(xT_sb, KC * b + KC)
                for n in range(n0, n0 + 2):
                    wait(pe, h_sb, NI * b + n - 1)
                    if n < 2:
                        wait(pe, (lg_done, rk_done)[n], b - 3)
                    for k in range(KC):
                        i_ = pe.matmul(bank[3 + n % 2][:, 0:C + 1], xT[:, k, n * P:(n + 1) * P], wx[:, k, :],
                                       start=(k == 0), stop=(k == KC - 1))
                    i_.then_inc(h_ps, 1)

            def spread_s2(front):
                q, s = front
                b = 2 * q + s
                pe.wait_ge(xT_sb, KC * b + KC)
                wait(pe, a_done, NI * b)
                for k in range(KC):
                    i_ = pe.matmul(bank[2][:, :], wa2r[:, k, :], xT[:, k, :], start=(k == 0), stop=(k == KC - 1))
                i_.then_inc(s2_ps, 1)

            def transpose_p(mid, i):
                q, s = mid
                g = NI * (2 * q + s) + i
                pe.wait_ge(p_done, g + 1)
                wait(pe, pt_sb, g - 1)
                for j in range(NI):
                    i_ = pe.transpose(bank[5 + i % 2][:, j * P:(j + 1) * P], pb[i % 2][:, j * P:(j + 1) * P], idf[:, :])
                i_.then_inc(pt_ps, 1)

            def attend(mid, i):
                q, s = mid
                g = NI * (2 * q + s) + i
                pe.wait_ge(pt_sb, g + 1)
                wait(pe, z_done, g)
                if isinstance(g, int) and g == 0:
                    pe.wait_ge(b1t_sb, 2)
                for j in range(NI):
                    i_ = pe.matmul(bank[7][:, 0:C], pT[i % 2][:, j, :], hs[s][:, j, 0:C],
                                   start=(j == 0), stop=(j == NI - 1))
                i_.then_inc(att_ps, 1)

            def transpose_x1(back):
                q, s = back
                b = 2 * q + s
                pe.wait_ge(xn2_done, NI * b + NI)
                for k in range(KC):
                    pe.wait_ge(xT_sb, min(KC * (b + 3) + k + 1, KC * B) if isinstance(b, int) else KC * (b + 3) + k + 1)
                    for n in range(NI):
                        i_ = pe.transpose(bank[k][:, n * P:(n + 1) * P], xn2[:, n, k * P:(k + 1) * P], idf[:, :])
                    i_.then_inc(t2_done, 1)

            def gate(back):
                q, s = back
                b = 2 * q + s
                pe.wait_ge(x2T_sb, KC * b + KC)
                pe.wait_ge(h_sb, min(NI * (b + 4), NI * B) if isinstance(b, int) else NI * (b + 4))
                for n in range(NI):
                    for k in range(KC):
                        i_ = pe.matmul(gate_ps[:, n * E:(n + 1) * E], x2T[:, k, n * P:(n + 1) * P], wg[:, k, :],
                                       start=(k == 0), stop=(k == KC - 1))
                i_.then_inc(gate_done, 1)

            def ranks(back):
                q, s = back
                b = 2 * q + s
                pe.wait_ge(m_done, b + 1)
                wait(pe, macc_done, b)
                wait(pe, rk_done, b)
                pe.matmul(rank_ps, tri[:, :], m16[:, :, :].rearrange("p n e -> p (n e)"), start=True, stop=False)
                for n in range(NI - 1):
                    pe.matmul(rank_ps[:, (n + 1) * E:].rearrange("p (n e) -> p n e", e=E), ones16[:, :],
                              m16[:, n:n + 1, :].broadcast_to((P, NI - 1 - n, E)), start=False, stop=False)
                pe.matmul(rank_ps.rearrange("p (n e) -> p n e", e=E), ones16[:, :],
                          macc[:, :].unsqueeze(1).broadcast_to((P, NI, E)), start=False, stop=True).then_inc(rank_done, 1)

            pe.wait_ge(consts, 2)
            pe.wait_ge(const_in, 16 * NCONST)
            pe.transpose(bank[7][:, 0:E * MT], xn2[0:E * MT, 0, 0:P], idf[0:E * MT, 0:E * MT]).then_inc(b1t_ps, 1)
            pe.wait_ge(wa_done, 7)
            graph_steps(pe, step)

            pe.wait_ge(macc_done, B)
            pe.matmul(bank[2][:, 0:E], ones16[:, :], macc[:, :], start=True, stop=True).then_inc(cnt_ps, 1)

            def transpose_rows(t, s):
                pe.wait_ge(xs_in[s], 16 * ((t - s) // 2 + 1) if isinstance(t, int) else t * 8 + (16 - 8 * s))
                wait(pe, xst_sb, t - 1)
                for j in range(JT):
                    for h in range(2):
                        for k in range(KC):
                            c = h * KC + k
                            i_ = pe.transpose(bank[s][:, :].bitcast(F16)[:, (c * JT + j) * P:(c * JT + j + 1) * P],
                                              xs[s][:, j, h * C + k * P:h * C + (k + 1) * P].bitcast(F16), idh[:, :])
                i_.then_inc(xst_ps, 1)

            def hidden(t, s, e):
                pe.wait_ge(xst_sb, t + 1)
                for m in range(FA):
                    wait(pe, act_done, FA * t - FA + m + 1 if not isinstance(t, int) or t > 0 else 0)
                    for half in range(2):
                        o = bank[2 + m][:, half * T:(half + 1) * T]
                        f = (half * FA + m) * P
                        terms = [(w1h, 0, 0), (w1h, 0, 1), (w1l, 0, 0)]
                        n_ = 0
                        for w, _, h in terms:
                            for k in range(KC):
                                i_ = pe.matmul(o, w[:, e * KC + k, f:f + P], xsT[s][:, h * KC + k, :],
                                               start=(n_ == 0), stop=(n_ == 3 * KC - 1))
                                n_ += 1
                    i_.then_inc(ag_ps, 1)

            def results(t, s, e):
                pe.wait_ge(al_done, FA * t + FA)
                wait(pe, yb_done, t - 1)
                for j in range(JT):
                    n_ = 0
                    for k in range(KF):
                        for a, w in ((ah, w2h), (ah, w2l), (al, w2h)):
                            i_ = pe.matmul(bank[6 + s][:, j * C:(j + 1) * C], a[s][:, k, j * P:(j + 1) * P],
                                           w[:, e * KF + k, :], start=(n_ == 0), stop=(n_ == 3 * KF - 1))
                            n_ += 1
                i_.then_inc(y_ps, 1)

            def expert(t):
                return pe.value_load(tabe[0:1, bass.ds(t, 1)], min_val=0, max_val=E - 1)

            pe.wait_ge(table, 3)
            transpose_rows(0, 0)
            hidden(0, 0, expert(0))
            transpose_rows(1, 1)
            hidden(1, 1, expert(1))
            transpose_rows(2, 0)
            results(0, 0, expert(0))
            hidden(2, 0, expert(2))
            transpose_rows(3, 1)
            results(1, 1, expert(1))
            with pe.Fori(1, (NT - 3) // 2) as j:
                hidden(2 * j + 1, 1, expert(2 * j + 1))
                transpose_rows(2 * j + 2, 0)
                results(2 * j, 0, expert(2 * j))
                hidden(2 * j + 2, 0, expert(2 * j + 2))
                transpose_rows(2 * j + 3, 1)
                results(2 * j + 1, 1, expert(2 * j + 1))
            t = NT - 3
            hidden(t + 1, 1, expert(t + 1))
            transpose_rows(t + 2, 0)
            results(t, 0, expert(t))
            hidden(t + 2, 0, expert(t + 2))
            results(t + 1, 1, expert(t + 1))
            results(t + 2, 0, expert(t + 2))

        @block.scalar
        def _(sc):
            act_ = nc.scalar.activation

            def step(G):
                for t in range(NI):
                    if t == 2 and G[0]:
                        q, s = G[0]
                        b = 2 * q + s
                        for k in range(KC):
                            sc.wait_ge(t1_done, KC * b + k + 1)
                            wait(sc, s2_ps, b)
                            act_(xT[:, k, :], bank[k][:, :], ACT.Copy).then_inc(xT_sb, 1)
                    if G[1]:
                        plus_s1(G[1], t)
                    if t == 3 and G[3]:
                        q, s = G[3]
                        b = 2 * q + s
                        for k in range(KC):
                            sc.wait_ge(t2_done, KC * b + k + 1)
                            wait(sc, gate_done, b)
                            act_(x2T[:, k, :], bank[k][:, :], ACT.Copy).then_inc(x2T_sb, 1)
                    if m := tile_at(G, t, 1):
                        probs(*m)
                    if t == 3 and G[2]:
                        q, s = G[2]
                        b = 2 * q + s
                        sc.wait_ge(z_done, NI * b + NI)
                        wait(sc, x1_done, b)
                        act_(ez[:, :, :], zb[s][:, :, :], ACT.Exp, bias=onesf[:, 0:1]).then_inc(ez_done, 1)
                    if m := tile_at(G, t, 2):
                        probs_t(*m)
                    if t == 0 and G[0]:
                        whi(2 * G[0][0] + G[0][1])
                    if t == 1 and G[4]:
                        q, s = G[4]
                        sc.wait_ge(d_done, 2 * q + s + 1)
                        act_(meta(rows[s], ED), meta(rows[s], ED), ACT.Exp).then_inc(ed_done, 1)
                    if t == 2 and G[3]:
                        q, s = G[3]
                        b = 2 * q + s
                        sc.wait_ge(xn2_done, NI * b + NI)
                        wait(sc, scattered[s], 16 * 2 * NI * q)
                        act_(rows[s][:, :, 0:C].bitcast(F16), xn2[:, :, :], ACT.Copy).then_inc(hi_done, 1)
                    if t >= 2 and G[0]:
                        q, s = G[0]
                        b = 2 * q + s
                        for n in range(2 * t - 4, 2 * t - 2):
                            sc.wait_ge(h_ps, NI * b + n + 1)
                            if n == 0:
                                wait(sc, att_ps, NI * (b - 1))
                                wait(sc, bh_done, b - 1)
                            act_(hs[s][:, n, :], bank[3 + n % 2][:, 0:C + 1], ACT.Copy).then_inc(h_sb, 1)

            def whi(b):
                sc.wait_ge(w_in, 32 * b + 32)
                sc.nop(nofuse=True)
                act_(w1h[:, b, :], wst1[:, :], ACT.Copy, scale=SW).then_inc(whi_done, 1)
                act_(w2h[:, bass.ds(b * KC, KC), :], wst2[:, :, :], ACT.Copy, scale=SW).then_inc(whi_done, 1)

            def plus_s1(mid, i):
                q, s = mid
                b = 2 * q + s
                g = NI * b + i
                sc.wait_ge(s2_ps, b + 1)
                sc.wait_ge(h_sb, NI * b + i + 1)
                wait(sc, em_done, g - 1)
                act_(at_s[i % 2][:, :], bank[2][:, :], ACT.Identity, bias=hs[s][:, i, C:C + 1]).then_inc(a_done, 1)

            def probs(mid, i):
                q, s = mid
                g = NI * (2 * q + s) + i
                sc.wait_ge(nm_done, g + 1)
                wait(sc, ri_done, g - 3)
                wait(sc, pt_ps, g - 1)
                act_(pb[i % 2][:, :], em[i % 2][:, :], ACT.Exp, bias=nmax[:, i % 2, :], accum_out=rsum[:, i, :]).then_inc(p_done, 1)

            def probs_t(mid, i):
                q, s = mid
                g = NI * (2 * q + s) + i
                sc.wait_ge(pt_ps, g + 1)
                wait(sc, att_ps, g - 1)
                act_(pT[i % 2][:, :, :], bank[5 + i % 2][:, :].rearrange("p (j r) -> p j r", j=NI), ACT.Copy).then_inc(pt_sb, 1)

            graph_steps(sc, step)

            sc.wait_ge(table, 3)

            def tile(t, s):
                e = sc.value_load(tabe[0:1, bass.ds(t, 1)], min_val=0, max_val=E - 1)
                for m in range(FA):
                    sc.wait_ge(ag_ps, FA * t + m + 1)
                    wait(sc, act_done, FA * t + m - 1)
                    sc.nop(nofuse=True)
                    act_(sil[m % 2][:, :], bank[2 + m][:, 0:T], ACT.Silu, bias=b1T[:, bass.ds(e * MT + m, 1)],
                         scale=1.0 / (SX * SW)).then_inc(sil_done, 1)
                    if m >= 1:
                        high(t, s, m - 1)
                high(t, s, FA - 1)

            def high(t, s, m):
                sc.wait_ge(act_done, FA * t + m + 1)
                if m == 0:
                    wait(sc, y_ps, t - 1)
                act_(ah[s][:, m, :], act[m % 2][:, :], ACT.Copy, scale=SA / (SX * SW)).then_inc(ah_done, 1)

            tile(0, 0)
            tile(1, 1)
            tile(2, 0)
            with sc.Fori(1, (NT - 1) // 2) as j:
                tile(2 * j + 1, 1)
                tile(2 * j + 2, 0)

        @block.vector
        def _(ve):
            ve.wait_ge(const_in, 16 * NCONST)
            for k in range(KC):
                ve.tensor_tensor_reduce(xn[:, k, :], wx[:, k, 0:C], av[:, 0:C], 1.0, 0.0, ALU.mult, ALU.add, wx[:, k, C:C + 1]).then_inc(wa_done, 1)
                ve.tensor_tensor_reduce(xn[:, 2 + k, :], wx[:, k, 0:C], av[:, C:2 * C], 1.0, 0.0, ALU.mult, ALU.add, wa2[:, k:k + 1]).then_inc(wa_done, 1)
            ve.wait_ge(wa_done, 4)
            ve.wait_ge(onesd, 5)
            for k in range(KC):
                i_ = ve.tensor_scalar(wa2r[:, k, :], onesf[:, :], wa2[:, k:k + 1], None, ALU.mult)
            i_.then_inc(wa_done, 1)
            ve.wait_ge(consts, 2)
            ve.tensor_copy(idh[:, :], idf[:, :])
            ve.tensor_copy(ones16[:, :], onesf[:, :])
            ve.tensor_copy(tri[:, :], trif[:, :]).then_inc(wa_done, 1)
            ve.wait_ge(b1t_ps, 1)
            ve.tensor_copy(b1T[:, :], bank[7][:, 0:E * MT]).then_inc(b1t_sb, 1)
            ve.tensor_scalar(b1S[:, :], bank[7][:, 0:E * MT], SX * SW, None, ALU.mult).then_inc(b1t_sb, 1)
            ve.wait_ge(b1t_sb, 2)
            ve.nop().then_inc(wa_done, 1)

            def step(G):
                for t in range(NI):
                    if m := tile_at(G, t, 4):
                        attended(*m)
                    if t == 0 and G[0]:
                        moments1(*G[0])
                    if t == 1 and G[0]:
                        q, s = G[0]
                        b = 2 * q + s
                        ve.wait_ge(rs1_done, b + 1)
                        wait(ve, t1_done, KC * b)
                        for n in range(NI):
                            ve.tensor_scalar(xn[:, n, :], xt[s][:, n, :], mv1[:, n, 0:1], rs1[:, n:n + 1], ALU.subtract, ALU.mult).then_inc(xn_done, 1)
                    if t == 2 and G[4]:
                        slots(G[4])
                    if t == 3 and G[2]:
                        q, s = G[2]
                        b = 2 * q + s
                        ve.wait_ge(xr_in[s], 16 * q + 16)
                        ve.wait_ge(z_done, NI * b + NI)
                        ve.scalar_tensor_tensor(xr[s][:, :, :], zb[s][:, :, :], -1.0, xr[s][:, :, :], ALU.max, ALU.add).then_inc(rl_done, 1)
                    if G[1]:
                        scores(G[1], t)
                    if t == 3 and G[2]:
                        q, s = G[2]
                        b = 2 * q + s
                        ve.wait_ge(ez_done, b + 1)
                        ve.wait_ge(rl_done, b + 1)
                        ve.scalar_tensor_tensor(xr[s][:, :, :], ez[:, :, :], 1.0, xr[s][:, :, :], ALU.min, ALU.add).then_inc(x1_done, 1)
                    if t == 0 and G[3]:
                        moments2(*G[3])
                    if t == 0 and G[4]:
                        top2(G[4])
                    if t == 1 and G[3]:
                        q, s = G[3]
                        b = 2 * q + s
                        ve.wait_ge(rs2_done, b + 1)
                        wait(ve, t2_done, KC * b)
                        wait(ve, lo_done, b)
                        wait(ve, hi_done, b)
                        for n in range(NI):
                            ve.tensor_scalar(xn2[:, n, :], xr[s][:, n, :], mv2[:, n, 0:1], rs2[:, n:n + 1], ALU.subtract, ALU.mult).then_inc(xn2_done, 1)
                    if t == 2 and G[3]:
                        q, s = G[3]
                        b = 2 * q + s
                        ve.wait_ge(hi_done, b + 1)
                        ve.wait_ge(xn2_done, NI * b + NI)
                        ve.tensor_tensor(rows[s][:, :, C:2 * C].bitcast(F16), xn2[:, :, :], rows[s][:, :, 0:C].bitcast(F16), ALU.subtract).then_inc(lo_done, 1)

            def moments1(q, s):
                b = 2 * q + s
                ve.wait_ge(x_in[s], 16 * q + 16)
                wait(ve, rs1_done, b)
                for n in range(NI):
                    ve.bn_stats(st1[:, n, :], xt[s][:, n, :]).then_inc(ln1_st, 1)
                ve.wait_ge(ln1_st, NI * b + NI)
                ve.nop(nofuse=True)
                for n in range(NI):
                    ve.bn_aggr(mv1[:, n, :], st1[:, n, :]).then_inc(ln1_mv, 1)

            def moments2(q, s):
                b = 2 * q + s
                ve.wait_ge(x1_done, b + 1)
                wait(ve, rs2_done, b)
                for n in range(NI):
                    ve.bn_stats(st2[:, n, :], xr[s][:, n, :]).then_inc(ln2_st, 1)
                ve.wait_ge(ln2_st, NI * b + NI)
                ve.nop(nofuse=True)
                for n in range(NI):
                    ve.bn_aggr(mv2[:, n, :], st2[:, n, :]).then_inc(ln2_mv, 1)

            def scores(mid, i):
                q, s = mid
                g = NI * (2 * q + s) + i
                ve.wait_ge(a_done, g + 1)
                ve.scalar_tensor_tensor(at_s[i % 2][:, :], at_s[i % 2][:, :], ALPHA, at_s[i % 2][:, :], ALU.mult, ALU.max).then_inc(lr_done, 1)
                ve.wait_ge(lr_done, g + 1)
                ve.wait_ge(consts, 4)
                wait(ve, p_done, g - 1)
                ve.nop(nofuse=True)
                ve.tensor_tensor_reduce(em[i % 2][:, :], at_s[i % 2][:, :], mask[:, i, :], 1.0, -3.0e38, ALU.mult, ALU.max, rmax[:, i % 2, :]).then_inc(em_done, 1)
                ve.wait_ge(em_done, g + 1)
                ve.tensor_scalar(nmax[:, i % 2, :], rmax[:, i % 2, :], -1.0, None, ALU.mult).then_inc(nm_done, 1)

            def attended(mid, i):
                q, s = mid
                b = 2 * q + s
                g = NI * b + i
                ve.wait_ge(p_done, g + 1)
                wait(ve, z_done, g - 1)
                ve.reciprocal(rinv[:, i % 2, :], rsum[:, i, :]).then_inc(ri_done, 1)
                ve.wait_ge(ri_done, g + 1)
                ve.wait_ge(att_ps, g + 1)
                ve.wait_ge(bh_done, b + 1)
                ve.scalar_tensor_tensor(zb[s][:, i, :], bank[7][:, 0:C], rinv[:, i % 2, :],
                                        zb[s][:, i, :], ALU.mult, ALU.add).then_inc(z_done, 1)

            def top2(back):
                q, s = back
                b = 2 * q + s
                ve.wait_ge(gate_done, b + 1)
                ve.scalar_tensor_tensor(lg[:, :, :], gate_ps.rearrange("p (n e) -> p n e", e=E), 1.0 / SX, bgb[:, :, :], ALU.mult, ALU.add).then_inc(lg_done, 1)
                ve.wait_ge(lg_done, b + 1)
                ve.nop(nofuse=True)
                for n in range(NI):
                    ve.max(mx[:, n, :], lg[:, n, :]).then_inc(mx_done, 1)
                ve.wait_ge(mx_done, NI * b + NI)
                ve.nop(nofuse=True)
                for n in range(NI):
                    ve.max_index(ix[:, n, :], mx[:, n, :], lg[:, n, :]).then_inc(ix_done, 1)
                ve.tensor_tensor(meta(rows[s], ED), mx[:, :, 1], mx[:, :, 0], ALU.subtract).then_inc(d_done, 1)
                ve.wait_ge(ix_done, NI * b + NI)
                ve.tensor_copy(ixf[:, :, :], ix[:, :, 0:2].rearrange("p n k -> p k n")).then_inc(ixf_done, 1)
                ve.wait_ge(ixf_done, b + 1)
                ve.tensor_tensor(oh[:, :, :], iota2[:, :, :], ixf[:, :, :].rearrange("p k n -> p (k n)").unsqueeze(2).broadcast_to((P, 2 * NI, E)), ALU.is_equal).then_inc(oh_done, 1)
                ve.wait_ge(oh_done, b + 1)
                wait(ve, rank_done, b)
                ve.tensor_tensor(m16[:, :, :], oh[:, 0:NI, :], oh[:, NI:2 * NI, :], ALU.add).then_inc(m_done, 1)

            def slots(back):
                q, s = back
                b = 2 * q + s
                ve.wait_ge(m_done, b + 1)
                ve.tensor_reduce(msum[:, :], m16[:, :, :].rearrange("p n e -> p e n"), AX, ALU.add).then_inc(msum_done, 1)
                ve.wait_ge(rank_done, b + 1)
                for k in range(2):
                    i_ = ve.tensor_tensor(rk[:, k * NI:(k + 1) * NI, :], oh[:, k * NI:(k + 1) * NI, :],
                                          rank_ps.rearrange("p (n e) -> p n e", e=E), ALU.mult)
                i_.then_inc(rk_done, 1)
                ve.wait_ge(msum_done, b + 1)
                ve.tensor_tensor(macc[:, :], macc[:, :], msum[:, :], ALU.add).then_inc(macc_done, 1)
                ve.tensor_copy(meta(rows[s], TOKEN, I32), tokc[s][:, :])
                ve.tensor_copy(meta(rows[s], E0), ixf[:, 0, :])
                ve.tensor_scalar(tokc[s][:, :], tokc[s][:, :], float(2 * N), None, ALU.add)
                ve.wait_ge(rk_done, b + 1)
                ve.tensor_reduce(rkr[:, :], rk[:, :, :], AX, ALU.add).then_inc(rkr_done, 1)
                ve.wait_ge(rkr_done, b + 1)
                wait(ve, scattered[s], 16 * 2 * NI * q)
                ve.scalar_tensor_tensor(slot[s][:, :], ixf[:, :, :].rearrange("p k n -> p (k n)"), float(R), rkr[:, :], ALU.mult, ALU.add).then_inc(slot_done, 1)

            graph_steps(ve, step)

            n_ = 0

            def then(i_):
                nonlocal n_
                i_.then_inc(tb, 1)
                n_ += 1
                ve.wait_ge(tb, n_)

            ve.wait_ge(cnt_ps, 1)
            then(ve.tensor_copy(cnt[:, :], bank[2][:, 0:E]))
            ve.tensor_copy(cnti[:, :], cnt[:, :]).then_inc(table, 1)
            ve.memset(one8[:, :], 1.0)
            then(ve.tensor_scalar(cntp[:, :], cnt[:, :], float(T - 1), None, ALU.add))
            then(ve.tensor_scalar(nti[:, :], cntp[:, :], T.bit_length() - 1, None, ALU.logical_shift_right))
            then(ve.tensor_copy(ntf[:, :], nti[:, :]))
            then(ve.tensor_tensor_scan(ends[:, :], one8[:, :], ntf[:, :], 0.0, ALU.mult, ALU.add))
            then(ve.tensor_tensor(ge[:, :, :], s_io[:, :].unsqueeze(2).broadcast_to((P, NT, E)), ends[:, :].unsqueeze(1).broadcast_to((P, NT, E)), ALU.is_ge))
            ve.tensor_reduce(ex[:, :], ge[:, :, :], AX, ALU.add)
            then(ve.tensor_tensor(gn[:, :, :], ge[:, :, :], ntf[:, :].unsqueeze(1).broadcast_to((P, NT, E)), ALU.mult))
            then(ve.tensor_reduce(stt[:, :], gn[:, :, :], AX, ALU.add))
            ve.tensor_scalar(tabe[:, :], ex[:, :], float(E - 1), None, ALU.min)
            then(ve.tensor_tensor(srow[:, :], s_io[:, :], stt[:, :], ALU.subtract))
            then(ve.tensor_scalar(srow[:, :], srow[:, :], float(T), None, ALU.mult))
            then(ve.scalar_tensor_tensor(srow[:, :], ex[:, :], float(R), srow[:, :], ALU.mult, ALU.add))
            then(ve.tensor_scalar(tabr[:, :], srow[:, :], float(E * R), None, ALU.min))
            ve.nop().then_inc(table, 2)

            def rows_t(t, s):
                ve.wait_ge(xst_ps, t + 1)
                wait(ve, ag_ps, FA * (t - 1))
                ve.tensor_copy(xsT[s][:, :, :].rearrange("p c r -> p (c r)"), bank[s][:, :].bitcast(F16)).then_inc(xst_sb, 1)

            def tile(t, s, more=True):
                e = ve.value_load(tabe[0:1, bass.ds(t, 1)], min_val=0, max_val=E - 1)
                for m in range(FA):
                    ve.wait_ge(sil_done, FA * t + m + 1)
                    wait(ve, ah_done, FA * t + m - 1)
                    wait(ve, al_done, FA * t + m - 1)
                    ve.scalar_tensor_tensor(act[m % 2][:, :], bank[2 + m][:, T:2 * T], b1S[:, bass.ds(e * MT + FA + m, 1)],
                                            sil[m % 2][:, :], ALU.add, ALU.mult).then_inc(act_done, 1)
                    if m >= 1:
                        low(t, s, m - 1)
                    if m == 1 and more:
                        rows_t(t + 1, 1 - s)
                low(t, s, FA - 1)
                row_weights(t, s)

            def row_weights(t, s):
                wait(ve, added[s], added_before(t, s))
                ve.tensor_copy(tok[s][:, :], meta(xs[s], TOKEN, I32))
                ve.tensor_scalar(wden[:, :], meta(xs[s], ED), 1.0, None, ALU.add).then_inc(wm, 1)
                ve.scalar_tensor_tensor(wsel[:, :], meta(xs[s], E0), ex[:, bass.ds(t, 1)], meta(xs[s], ED), ALU.is_equal, ALU.max).then_inc(wm, 1)
                ve.wait_ge(wm, 3 * t + 2)
                ve.reciprocal(winv[:, :], wden[:, :]).then_inc(wm, 1)
                ve.wait_ge(wm, 3 * t + 3)
                ve.tensor_tensor(wrow[s][:, :], wsel[:, :], winv[:, :], ALU.mult).then_inc(wrow_done, 1)

            def added_before(t, s):
                return 16 * JT * ((t - s) // 2) if isinstance(t, int) else t * (8 * JT) - 8 * JT * s

            def low(t, s, m):
                ve.wait_ge(ah_done, FA * t + m + 1)
                ve.wait_ge(act_done, FA * t + m + 1)
                ve.scalar_tensor_tensor(al[s][:, m, :], act[m % 2][:, :], SA / (SX * SW), ah[s][:, m, :], ALU.mult, ALU.subtract).then_inc(al_done, 1)

            def result(t, s):
                e = ve.value_load(tabe[0:1, bass.ds(t, 1)], min_val=0, max_val=E - 1)
                ve.wait_ge(y_ps, t + 1)
                wait(ve, added[s], added_before(t, s))
                ve.scalar_tensor_tensor(ys[s][:, :, :], bank[6 + s][:, :].rearrange("p (j c) -> p j c", j=JT), 1.0 / (SA * SW),
                                        b2b[:, bass.ds(e, 1), :].broadcast_to((P, JT, C)), ALU.mult, ALU.add).then_inc(yb_done, 1)
                ve.wait_ge(yb_done, t + 1)
                ve.wait_ge(wrow_done, t + 1)
                for j in range(JT):
                    i_ = ve.tensor_scalar(ys[s][:, j, :], ys[s][:, j, :], wrow[s][:, j:j + 1], None, ALU.mult)
                i_.then_inc(y_sb, 1)

            rows_t(0, 0)
            tile(0, 0)
            tile(1, 1)
            result(0, 0)
            tile(2, 0)
            result(1, 1)
            tile(3, 1)
            result(2, 0)
            with ve.Fori(2, (NT - 1) // 2) as j:
                tile(2 * j, 0)
                result(2 * j - 1, 1)
                tile(2 * j + 1, 1)
                result(2 * j, 0)
            tile(NT - 1, 0, more=False)
            result(NT - 2, 1)
            result(NT - 1, 0)


_INS = ['x', 'adj', 'L0_gnn_W', 'L0_gnn_a', 'L0_gnn_beta', 'L0_ffn_Wg', 'L0_ffn_bg', 'L0_ffn_W1', 'L0_ffn_b1', 'L0_ffn_W2', 'L0_ffn_b2']
_OUTS = [((16, 512, 256), 'float32')]


def kernel(**inputs):
    import numpy as _np
    import concourse.bacc as _bacc
    from concourse import mybir as _mybir
    from concourse.bass_utils import run_bass_kernel_spmd as _run

    nc = _bacc.Bacc("TRN2", target_bir_lowering=False, num_devices=1)
    arrays, args = {}, []
    for name in _INS:
        a = _np.ascontiguousarray(inputs[name])
        arrays[f"in_{name}_dram"] = a
        args.append(nc.dram_tensor(f"in_{name}_dram", a.shape, _mybir.dt.from_np(a.dtype), kind="ExternalInput").ap())
    for i, (shape, dtype) in enumerate(_OUTS):
        dt = _mybir.dt.from_np(_np.dtype(dtype))
        args.append(nc.dram_tensor(f"out_{i}_dram", shape, dt, kind="ExternalOutput").ap())
    build_gat_moe(nc, *args)
    r = _run(nc, [arrays], core_ids=[0])
    return r.results[0]["out_0_dram"]
```

```python
from contextlib import ExitStack

import concourse.bass as bass
from concourse import mybir

F32 = mybir.dt.float32
F16 = mybir.dt.float16
BF16 = mybir.dt.bfloat16
I32 = mybir.dt.int32
U32 = mybir.dt.uint32
ALU = mybir.AluOpType
ACT = mybir.ActivationFunctionType
AX = mybir.AxisListType.X

P = 128
T = 256
JT = T // P
SX = 16.0
SW = 64.0
SA = 16.0
EPS = 1e-5
ALPHA = 0.2


def wait(eng, semaphore, value):
    if not isinstance(value, int) or value >= 1:
        eng.wait_ge(semaphore, value)


def build_gat_moe(nc, x, adj, gW, ga, gbeta, Wg, bg, W1, b1, W2, b2, out):
    B, N, C = x.shape
    NI = N // P
    KC = C // P
    E = Wg.shape[1]
    DFF = W2.shape[1]
    FA = DFF // P
    H1 = 2 * DFF
    MT = H1 // P
    KF = DFF // P
    TOK = B * N
    NT = 2 * TOK // T + E - 1
    R = TOK + T
    NCH = E * KC
    assert NCH == B and KC == 2 and KF == 2 * KC and NT % 2 == 1

    x_v = x.rearrange("b (p n) c -> b p n c", n=NI)
    adj_v = adj.rearrange("(p n) j -> p n j", n=NI)
    W1_v = W1.rearrange("e (k p) f -> (e k) p f", p=P)
    W2_v = W2.rearrange("e (a k p) c -> (e a) p k c", p=P, k=KC)

    RW = C + 4
    TOKEN, ED, E0 = C, C + 1, C + 2
    rows_d = nc.dram_tensor("expert_rows", (E * R + T, RW), F32, kind="Internal").ap()
    acc_d = out
    assert out.shape[0] == TOK + T
    x1_v = acc_d[0:TOK, :].rearrange("(b p n) c -> b p n c", p=P, n=NI)

    def tile_of(rows):
        return rows.rearrange("(p j) c -> p j c", j=JT)

    def meta(t, k, dt=F32):
        return t[:, :, k:k + 1].bitcast(dt)[:, :, 0]

    at = [(nc.sbuf_base + 31) // 32 * 32]

    def sb(name, shape, dt):
        size = mybir.dt.size(dt)
        for d in shape[1:]:
            size *= d
        t = nc.alloc_sbuf_tensor_at(name, list(shape), dt, offset=at[0])
        at[0] += (size + 31) // 32 * 32
        assert at[0] <= nc.sbuf_usable_end, (name, at[0])
        return t

    w1h = sb("w1h", [P, E * KC, H1], F16)
    w1l = sb("w1l", [P, E * KC, H1], F16)
    w2h = sb("w2h", [P, E * KF, C], F16)
    w2l = sb("w2l", [P, E * KF, C], F16)
    b1T = sb("b1T", [P, E * MT], F32)
    b1S = sb("b1S", [P, E * MT], F32)
    b2b = sb("b2b", [P, E, C], F32)
    pad = sb("pad", [P, JT, RW], F32)
    s_io = sb("s_io", [P, NT], F32)
    macc = sb("macc", [P, E], BF16)
    warm = sb("warm", [P, 1], F32)
    ones16 = sb("ones16", [P, P], BF16)
    idf = sb("idf", [P, P], F32)
    phase = at[0]

    wst1 = sb("wst1", [P, H1], F32)
    wst2 = sb("wst2", [P, KC, C], F32)
    xt = [sb(f"xt{i}", [P, NI, C], F32) for i in range(2)]
    xn = sb("xn", [P, NI, C], F32)
    xT = sb("xT", [P, KC, N], F32)
    tokc = [sb(f"tokc{i}", [P, NI], F32) for i in range(2)]
    b1n = sb("b1n", [E * MT, P], F32)
    onesf = sb("onesf", [P, P], F32)
    tri = sb("tri", [P, P], BF16)
    trif = sb("trif", [P, P], F32)
    wx = sb("wx", [P, KC, C + 1], F32)
    av = sb("av", [P, 2 * C], F32)
    wa2 = sb("wa2", [P, KC], F32)
    wa2r = sb("wa2r", [P, KC, P], F32)
    betat = sb("betat", [P, 1], F32)
    bgb = sb("bgb", [P, NI, E], F32)
    wg = sb("wg", [P, KC, E], F32)
    iota2 = sb("iota2", [P, 2 * NI, E], F32)
    halfs = sb("halfs", [P, NI], F32)
    mask = sb("mask", [P, NI, N], F32)
    xr = [sb(f"xr{i}", [P, NI, C], F32) for i in range(2)]
    xn2 = [sb(f"xn2{i}", [P, NI, RW], F32) for i in range(2)]
    x2T = sb("x2T", [P, KC, N], F32)
    hs = [sb(f"hs{i}", [P, NI, C + 1], F32) for i in range(2)]
    zb = [sb(f"zb{i}", [P, NI, C], F32) for i in range(2)]
    ez = sb("ez", [P, NI, C], F32)
    at_s = [sb(f"at_s{i}", [P, N], F32) for i in range(2)]
    em = [sb(f"em{i}", [P, N], F32) for i in range(2)]
    pb = [sb(f"pb{i}", [P, N], F32) for i in range(2)]
    pT = [sb(f"pT{i}", [P, NI, P], F32) for i in range(2)]
    st1 = sb("st1", [P, NI, 6], F32)
    mv1 = sb("mv1", [P, NI, 2], F32)
    st2 = sb("st2", [P, NI, 6], F32)
    mv2 = sb("mv2", [P, NI, 2], F32)
    ve1 = sb("ve1", [P, NI], F32)
    ve2 = sb("ve2", [P, NI], F32)
    rs1 = sb("rs1", [P, NI], F32)
    nm1 = sb("nm1", [P, NI], F32)
    rs2 = sb("rs2", [P, NI], F32)
    rmax = sb("rmax", [P, 2, 1], F32)
    nmax = sb("nmax", [P, 2, 1], F32)
    rsum = sb("rsum", [P, 4, 1], F32)
    rinv = sb("rinv", [P, 2, 1], F32)
    lg = sb("lg", [P, NI, E], F32)
    mx = sb("mx", [P, NI, E], F32)
    ix = sb("ix", [P, NI, E], U32)
    ixf = sb("ixf", [P, 2, NI], F32)
    oh = sb("oh", [P, 2 * NI, E], F32)
    m16 = sb("m16", [P, NI, E], BF16)
    msum = sb("msum", [P, E], F32)
    rk = sb("rk", [P, 2 * NI, E], F32)
    rkr = sb("rkr", [P, 2 * NI], F32)
    slot = [sb(f"slot{i}", [P, 2 * NI], I32) for i in range(2)]

    at[0] = phase
    cnt = sb("cnt", [P, E], F32)
    cnti = sb("cnti", [P, E], I32)
    cntp = sb("cntp", [P, E], I32)
    nti = sb("nti", [P, E], I32)
    ntf = sb("ntf", [P, E], F32)
    one8 = sb("one8", [P, E], F32)
    ends = sb("ends", [P, E], F32)
    ge = sb("ge", [P, NT, E], F32)
    gn = sb("gn", [P, NT, E], F32)
    ex = sb("ex", [P, NT], F32)
    stt = sb("stt", [P, NT], F32)
    srow = sb("srow", [P, NT], F32)
    tabe = sb("tabe", [P, NT], I32)
    tabr = sb("tabr", [P, NT], I32)
    xs = [sb(f"xs{i}", [P, JT, RW], F32) for i in range(2)]
    xsT = [sb(f"xsT{i}", [P, 2 * KC, T], F16) for i in range(2)]
    sil = [sb(f"sil{i}", [P, T], F32) for i in range(2)]
    act = [sb(f"act{i}", [P, T], F32) for i in range(2)]
    ah = [sb(f"ah{i}", [P, KF, T], F16) for i in range(2)]
    al = [sb(f"al{i}", [P, KF, T], F16) for i in range(2)]
    ys = [sb(f"ys{i}", [P, JT, C], F32) for i in range(2)]
    tok = [sb(f"tok{i}", [P, JT], I32) for i in range(2)]
    wden = sb("wden", [P, JT], F32)
    wsel = sb("wsel", [P, JT], F32)
    winv = sb("winv", [P, JT], F32)
    wrow = [sb(f"wrow{i}", [P, JT], F32) for i in range(2)]

    with ExitStack() as ctx:
        bank = [ctx.enter_context(nc.psum_tensor(f"bank{i}", [P, 512], F32)) for i in range(8)]
        gate_ps = bank[3][:, 0:NI * E]
        rank_ps = bank[7][:, C:C + NI * E], bank[4][:, 0:NI * E]

        def sem(name):
            return ctx.enter_context(nc.semaphore(name))

        gnn_in = sem("gnn_in")
        rest_in = sem("rest_in")
        x_in = [sem(f"x_in{i}") for i in range(2)]
        xr_in = [sem(f"xr_in{i}") for i in range(2)]
        w_in = sem("w_in")
        adj_in = sem("adj_in")
        x1_out = [sem(f"x1_out{i}") for i in range(2)]
        scattered = [sem(f"scattered{i}") for i in range(2)]
        consts = sem("consts")
        masked = sem("masked")
        onesd = sem("onesd")
        wa_done = sem("wa_done")
        b1t_ps = sem("b1t_ps")
        b1t_sb = sem("b1t_sb")
        ln1_st = sem("ln1_st")
        ln1_mv = sem("ln1_mv")
        ve1_done = sem("ve1_done")
        rs1_done = sem("rs1_done")
        nm1_done = sem("nm1_done")
        xn_done = sem("xn_done")
        t1_done = sem("t1_done")
        xT_sb = sem("xT_sb")
        h_ps = sem("h_ps")
        h_sb = sem("h_sb")
        s2_ps = sem("s2_ps")
        bh_done = sem("bh_done")
        a_done = sem("a_done")
        lr_done = sem("lr_done")
        em_done = sem("em_done")
        nm_done = sem("nm_done")
        p_done = sem("p_done")
        pt_ps = sem("pt_ps")
        pt_sb = sem("pt_sb")
        att_ps = sem("att_ps")
        ri_done = sem("ri_done")
        z_done = sem("z_done")
        ez_done = sem("ez_done")
        rl_done = sem("rl_done")
        x1_done = sem("x1_done")
        ln2_st = sem("ln2_st")
        ln2_mv = sem("ln2_mv")
        ve2_done = sem("ve2_done")
        rs2_done = sem("rs2_done")
        xn2_done = sem("xn2_done")
        t2_done = sem("t2_done")
        x2T_sb = sem("x2T_sb")
        gate_done = sem("gate_done")
        lg_done = sem("lg_done")
        mx_done = sem("mx_done")
        ix_done = sem("ix_done")
        ixf_done = sem("ixf_done")
        oh_done = sem("oh_done")
        m_done = sem("m_done")
        rank_done = sem("rank_done")
        msum_done = sem("msum_done")
        macc_done = sem("macc_done")
        rk_done = sem("rk_done")
        rkr_done = sem("rkr_done")
        slot_done = sem("slot_done")
        d_done = sem("d_done")
        ed_done = sem("ed_done")
        whi_done = sem("whi_done")
        wsc_done = sem("wsc_done")
        wlo_done = sem("wlo_done")
        cnt_ps = sem("cnt_ps")
        tb = sem("tb")
        table = sem("table")
        zdone = sem("zdone")
        padc = sem("padc")
        xs_in = [sem(f"xs_in{i}") for i in range(2)]
        xst_ps = sem("xst_ps")
        xhi_done = sem("xhi_done")
        xlo_done = sem("xlo_done")
        ag_ps = sem("ag_ps")
        sil_done = sem("sil_done")
        act_done = sem("act_done")
        ah_done = sem("ah_done")
        al_done = sem("al_done")
        y_ps = sem("y_ps")
        y_sb = sem("y_sb")
        wm = sem("wm")
        wrow_done = sem("wrow_done")
        yb_done = sem("yb_done")
        added = [sem(f"added{i}") for i in range(2)]

        REST = 3 + NI
        adj_nat = [xr[i][:, :, :].rearrange("p n c -> p (n c)").rearrange("p (n j) -> p n j", j=N) for i in range(2)]
        block = ctx.enter_context(nc.Block())

        LAGS = 5
        LAST = B + LAGS - 1

        def graph_steps(eng, step, tail=0):
            def one(i):
                step([((i - lag) // 2, (i - lag) % 2) if 0 <= i - lag < B else None for lag in range(LAGS)])
            for i in range(6):
                one(i)
            with eng.Fori(3, (B - tail) // 2) as j:
                for u in range(2):
                    step([(j + (u - lag) // 2, (u - lag) % 2) for lag in range(LAGS)])
            for i in range(B - tail, LAST):
                one(i)

        def tile_at(G, t, lag):
            g = G[1] if t >= lag else G[2]
            return g and (g, (t - lag) % NI)

        def next_graph(G):
            if not G[0]:
                return None
            q, s = G[0]
            return (q + s, 1 - s) if not isinstance(q, int) or 2 * q + s + 1 < B else None

        def late(G):
            return not G[1]

        @block.sync
        def _(sp):
            sp.dma_start(xt[0][:, :, :], x_v[0]).then_inc(x_in[0], 16)
            sp.dma_start(av[:, :], ga.rearrange("f o -> (f o)").partition_broadcast(P)).then_inc(gnn_in, 16)

            def more_constants():
                for i in range(2):
                    sp.dma_start(adj_nat[i], adj_v[:, 2 * i:2 * i + 2, :]).then_inc(adj_in, 16)
                sp.dma_start(wg[:, :, :], Wg.rearrange("(k p) e -> p k e", p=P)).then_inc(rest_in, 16)
                for n in range(NI):
                    sp.dma_start(bgb[:, n, :], bg.partition_broadcast(P)).then_inc(rest_in, 16)
                sp.dma_start(b1n[:, :], b1.rearrange("e (m p) -> (e m) p", p=P)).then_inc(rest_in, 16)
                sp.dma_start(b2b[:, :, :], b2.rearrange("e c -> (e c)").partition_broadcast(P)).then_inc(rest_in, 16)

            def padding():
                sp.wait_ge(padc, 3)
                sp.dma_start(tile_of(rows_d[E * R:E * R + T, :]), pad[:, :, :]).then_inc(zdone, 16)
                sp.dma_start(tile_of(acc_d[TOK:TOK + T, :]), pad[:, :, 0:C]).then_inc(zdone, 16)

            def step(G):
                if G[0]:
                    q, s = G[0]
                    b = 2 * q + s
                    if not isinstance(b, int) or b + 1 < B:
                        wait(sp, xn_done, NI * b)
                        sp.dma_start(xt[1 - s][:, :, :], x_v[b + 1]).then_inc(x_in[1 - s], 16)
                    wait(sp, wlo_done, 2 * b)
                    sp.dma_start(wst1[:, :], W1_v[b]).then_inc(w_in, 16)
                    sp.dma_start(wst2[:, :, :], W2_v[b]).then_inc(w_in, 16)
                    if isinstance(b, int) and b == 0:
                        more_constants()
                    if isinstance(b, int) and b == 1:
                        padding()
                if G[3]:
                    q, s = G[3]
                    b = 2 * q + s
                    sp.wait_ge(x1_done, b + 1)
                    sp.dma_start(x1_v[b], xr[s][:, :, :]).then_inc(x1_out[s], 16)
                if G[1]:
                    q, s = G[1]
                    b = 2 * q + s
                    if not isinstance(q, int) or q >= 1:
                        sp.wait_ge(x1_out[s], 16 * q)
                        sp.wait_ge(xn2_done, (b - 1) * NI)
                    else:
                        sp.wait_ge(masked, 2)
                    sp.dma_start(xr[s][:, :, :], x_v[b]).then_inc(xr_in[s], 16)

            graph_steps(sp, step, tail=2)

            sp.wait_ge(table, 1)
            for e in range(E):
                c_e = sp.value_load(cnti[0:1, e:e + 1], min_val=0, max_val=TOK)
                sp.dma_start(tile_of(rows_d[bass.ds(c_e + e * R, T), :]), pad[:, :, :]).then_inc(zdone, 16)
            def first_row(t):
                return sp.value_load(tabr[0:1, bass.ds(t, 1)], min_val=0, max_val=E * R)

            sp.wait_ge(table, 3)
            first_rows = [first_row(t) for t in range(2)]
            sp.wait_ge(zdone, 16 * (E + 2))
            for s in range(2):
                sp.wait_ge(scattered[s], 16 * 2 * NI * (B // 2))
                sp.wait_ge(x1_out[s], 16 * (B // 2))

            def load_rows(r, s):
                sp.dma_start(xs[s][:, :, :], tile_of(rows_d[bass.ds(r, T), :])).then_inc(xs_in[s], 16)

            for s in range(2):
                load_rows(first_rows[s], s)
            with sp.Fori(0, (NT - 3) // 2) as j:
                for s in range(2):
                    sp.wait_ge(xst_ps, 2 * j + s + 1)
                    sp.wait_ge(wrow_done, 2 * j + s + 1)
                    load_rows(first_row(2 * j + s + 2), s)
            sp.wait_ge(xst_ps, NT - 2)
            sp.wait_ge(wrow_done, NT - 2)
            load_rows(first_row(NT - 1), 0)
            sp.wait_ge(added[0], 16 * JT * ((NT + 1) // 2))
            sp.wait_ge(added[1], 16 * JT * (NT // 2))
        @block.gpsimd
        def _(pool):
            pool.memset(warm[:, :], 0.0)
            pool.memset(onesf[:, :], 1.0).then_inc(onesd, 1)
            pool.memset(halfs[:, :], -0.5).then_inc(onesd, 1)
            pool.memset(macc[:, :], 0.0).then_inc(onesd, 1)
            pool.iota(iota2[:, :, :], pattern=[[0, 2 * NI], [1, E]], base=0, channel_multiplier=0, allow_small_or_imprecise_dtypes=True).then_inc(onesd, 1)
            for s in range(2):
                pool.iota(tokc[s][:, :], pattern=[[1, NI]], base=s * N, channel_multiplier=NI, allow_small_or_imprecise_dtypes=True)
            pool.iota(s_io[:, :], pattern=[[1, NT]], base=0, channel_multiplier=0, allow_small_or_imprecise_dtypes=True).then_inc(onesd, 1)
            for s in range(2):
                pool.memset(xn2[s][:, :, C:RW], 0.0)
            pool.wait_ge(onesd, 5)
            pool.affine_select(idf[:, :], onesf[:, :], pattern=[[-1, P]], compare_op=ALU.is_equal, fill=0.0, base=0, channel_multiplier=1).then_inc(consts, 1)

            def rstd1(q, s):
                b = 2 * q + s
                pool.wait_ge(ln1_mv, NI * b + NI)
                pool.nop(nofuse=True)
                pool.tensor_scalar(ve1[:, :], mv1[:, :, 1], 1.0, EPS, ALU.mult, ALU.add).then_inc(ve1_done, 1)
                pool.wait_ge(ve1_done, b + 1)
                wait(pool, xn_done, NI * b)
                pool.tensor_tensor(rs1[:, :], ve1[:, :], halfs[:, :], ALU.pow).then_inc(rs1_done, 1)

            rstd1(0, 0)
            pool.affine_select(trif[:, :], onesf[:, :], pattern=[[1, P]], compare_op=ALU.is_gt, fill=0.0, base=0, channel_multiplier=-1).then_inc(consts, 1)
            pool.wait_ge(adj_in, 32)
            for n in range(NI):
                src = adj_nat[n // 2][:, n % 2, :].rearrange("p (q m) -> p m q", m=NI)
                i_ = pool.tensor_scalar(mask[:, n, :].rearrange("p (m q) -> p m q", m=NI), src, 1.0, 1.0, ALU.mult, ALU.mult)
                if n % 2:
                    i_.then_inc(masked, 1)
            rstd1(0, 1)
            pool.memset(pad[:, :, :], 0.0).then_inc(padc, 1)
            pool.wait_ge(padc, 1)
            pool.iota(meta(pad, TOKEN, I32), pattern=[[1, JT]], base=TOK, channel_multiplier=JT).then_inc(padc, 2)
            pool.wait_ge(gnn_in, 16 * 3)

            def step(G):
                if G[1]:
                    q, s = G[1]
                    b = 2 * q + s
                    pool.wait_ge(h_sb, NI * b + NI)
                    wait(pool, rl_done, b - 1)
                    wait(pool, ez_done, b - 1)
                    pool.nop(nofuse=True)
                    pool.tensor_scalar(zb[s][:, :, :], hs[s][:, :, 0:C], betat[:, 0:1], -1.0, ALU.mult, ALU.add).then_inc(bh_done, 1)
                if G[3]:
                    q, s = G[3]
                    b = 2 * q + s
                    pool.wait_ge(ln2_mv, NI * b + NI)
                    pool.nop(nofuse=True)
                    pool.tensor_scalar(ve2[:, :], mv2[:, :, 1], EPS, 1.0 / (SX * SX), ALU.add, ALU.mult).then_inc(ve2_done, 1)
                    pool.wait_ge(ve2_done, b + 1)
                    wait(pool, xn2_done, NI * b)
                    pool.tensor_tensor(rs2[:, :], ve2[:, :], halfs[:, :], ALU.pow).then_inc(rs2_done, 1)
                if G[0]:
                    q, s = G[0]
                    b = 2 * q + s
                    pool.wait_ge(whi_done, 2 * b + 2)
                    pool.nop(nofuse=True)
                    pool.tensor_scalar(wst1[:, :], wst1[:, :], SW, 1.0, ALU.mult, ALU.mult).then_inc(wsc_done, 1)
                    pool.tensor_scalar(wst2[:, :, :], wst2[:, :, :], SW, 1.0, ALU.mult, ALU.mult).then_inc(wsc_done, 1)
                if next_graph(G) and not G[4] and G[1]:
                    rstd1(*next_graph(G))
                if G[0]:
                    q, s = G[0]
                    b = 2 * q + s
                    pool.wait_ge(wsc_done, 2 * b + 2)
                    pool.nop(nofuse=True)
                    pool.tensor_tensor(w1l[:, b, :], wst1[:, :], w1h[:, b, :], ALU.subtract).then_inc(wlo_done, 1)
                    pool.tensor_tensor(w2l[:, bass.ds(b * KC, KC), :], wst2[:, :, :], w2h[:, bass.ds(b * KC, KC), :], ALU.subtract).then_inc(wlo_done, 1)
                if next_graph(G) and G[4]:
                    rstd1(*next_graph(G))
                if G[4]:
                    q, s = G[4]
                    b = 2 * q + s
                    pool.wait_ge(slot_done, b + 1)
                    pool.wait_ge(xn2_done, NI * b + NI)
                    pool.wait_ge(ed_done, b + 1)
                    pool.nop(nofuse=True)
                    for k in range(2):
                        for n in range(NI):
                            pool.indirect_dma_start(
                                out=rows_d, out_offset=bass.IndirectOffsetOnAxis(ap=slot[s][:, k * NI + n:k * NI + n + 1], axis=0),
                                in_=xn2[s][:, n, :], in_offset=None).then_inc(scattered[s], 16)

            graph_steps(pool, step, tail=2)

            def add(t, s, before):
                pool.wait_ge(y_sb, t + 1)
                wait(pool, added[1 - s], 16 * JT * before)
                pool.nop(nofuse=True)
                for j in range(JT):
                    pool.indirect_dma_start(
                        out=acc_d, out_offset=bass.IndirectOffsetOnAxis(ap=tok[s][:, j:j + 1], axis=0),
                        in_=ys[s][:, j, :], in_offset=None, compute_op=ALU.add).then_inc(added[s], 16)

            for s in range(2):
                pool.wait_ge(x1_out[s], 16 * (B // 2))
            add(0, 0, 0)
            add(1, 1, 1)
            with pool.Fori(1, (NT - 1) // 2) as j:
                add(2 * j, 0, j)
                add(2 * j + 1, 1, j + 1)
            add(NT - 1, 0, NT // 2)

        @block.tensor
        def _(pe):
            def step(G):
                for t in range(NI):
                    if t == 2 and G[4] and not late(G):
                        ranks(G[4], rank_ps[0])
                    if m := tile_at(G, t, 3):
                        attend(*m)
                    if m := tile_at(G, t, 2):
                        transpose_p(*m)
                    if t == 1 and G[4] and late(G):
                        ranks(G[4], rank_ps[1])
                    if t == 0 and G[4]:
                        gate(G[4])
                    if t == 1 and G[0]:
                        transpose_x(G[0])
                    if t == 2 and G[0]:
                        project(G[0], 0)
                        spread_s2(G[0])
                    if t == 3 and G[3]:
                        transpose_x1(G[3])
                    if t == 3 and G[0]:
                        project(G[0], 2)

            def transpose_x(front):
                q, s = front
                b = 2 * q + s
                pe.wait_ge(xn_done, NI * b + NI)
                for k in range(KC):
                    wait(pe, x2T_sb, KC * (b - 4) + k + 1)
                    for n in range(NI):
                        i_ = pe.transpose(bank[k][:, n * P:(n + 1) * P], xn[:, n, k * P:(k + 1) * P], idf[:, :])
                    i_.then_inc(t1_done, 1)

            def project(front, n0):
                q, s = front
                b = 2 * q + s
                pe.wait_ge(xT_sb, KC * b + KC)
                for n in range(n0, n0 + 2):
                    wait(pe, h_sb, NI * b + n - 1)
                    if n == 0:
                        wait(pe, lg_done, b - 3)
                    for k in range(KC):
                        i_ = pe.matmul(bank[3 + n % 2][:, 0:C + 1], xT[:, k, n * P:(n + 1) * P], wx[:, k, :],
                                       start=(k == 0), stop=(k == KC - 1))
                    i_.then_inc(h_ps, 1)

            def spread_s2(front):
                q, s = front
                b = 2 * q + s
                pe.wait_ge(xT_sb, KC * b + KC)
                wait(pe, a_done, NI * b)
                for k in range(KC):
                    i_ = pe.matmul(bank[2][:, :], wa2r[:, k, :], xT[:, k, :], start=(k == 0), stop=(k == KC - 1))
                i_.then_inc(s2_ps, 1)

            def transpose_p(mid, i):
                q, s = mid
                g = NI * (2 * q + s) + i
                pe.wait_ge(p_done, g + 1)
                wait(pe, pt_sb, g - 1)
                for j in range(NI):
                    i_ = pe.transpose(bank[5 + i % 2][:, j * P:(j + 1) * P], pb[i % 2][:, j * P:(j + 1) * P], idf[:, :])
                i_.then_inc(pt_ps, 1)

            def attend(mid, i):
                q, s = mid
                g = NI * (2 * q + s) + i
                pe.wait_ge(pt_sb, g + 1)
                wait(pe, z_done, g)
                for j in range(NI):
                    i_ = pe.matmul(bank[7][:, 0:C], pT[i % 2][:, j, :], hs[s][:, j, 0:C],
                                   start=(j == 0), stop=(j == NI - 1))
                i_.then_inc(att_ps, 1)

            def transpose_x1(back):
                q, s = back
                b = 2 * q + s
                pe.wait_ge(xn2_done, NI * b + NI)
                for k in range(KC):
                    pe.wait_ge(xT_sb, min(KC * (b + 3) + k + 1, KC * B) if isinstance(b, int) else KC * (b + 3) + k + 1)
                    for n in range(NI):
                        i_ = pe.transpose(bank[k][:, n * P:(n + 1) * P], xn2[s][:, n, k * P:(k + 1) * P], idf[:, :])
                    i_.then_inc(t2_done, 1)

            def gate(back):
                q, s = back
                b = 2 * q + s
                pe.wait_ge(x2T_sb, KC * b + KC)
                if isinstance(b, int) and b == 0:
                    pe.wait_ge(rest_in, 16 * REST)
                pe.wait_ge(h_sb, min(NI * (b + 4), NI * B) if isinstance(b, int) else NI * (b + 4))
                for n in range(NI):
                    for k in range(KC):
                        i_ = pe.matmul(gate_ps[:, n * E:(n + 1) * E], x2T[:, k, n * P:(n + 1) * P], wg[:, k, :],
                                       start=(k == 0), stop=(k == KC - 1))
                i_.then_inc(gate_done, 1)

            def ranks(back, ps):
                q, s = back
                b = 2 * q + s
                pe.wait_ge(m_done, b + 1)
                if isinstance(b, int) and b == 0:
                    pe.wait_ge(wa_done, 6)
                wait(pe, macc_done, b)
                wait(pe, rk_done, b)
                if ps is rank_ps[0]:
                    pe.wait_ge(z_done, min(NI * (b + 2) + 3, NI * B) if isinstance(b, int) else NI * (b + 2) + 3)
                pe.matmul(ps, tri[:, :], m16[:, :, :].rearrange("p n e -> p (n e)"), start=True, stop=False)
                for n in range(NI - 1):
                    pe.matmul(ps[:, (n + 1) * E:].rearrange("p (n e) -> p n e", e=E), ones16[:, :],
                              m16[:, n:n + 1, :].broadcast_to((P, NI - 1 - n, E)), start=False, stop=False)
                pe.matmul(ps.rearrange("p (n e) -> p n e", e=E), ones16[:, :],
                          macc[:, :].unsqueeze(1).broadcast_to((P, NI, E)), start=False, stop=True).then_inc(rank_done, 1)

            pe.wait_ge(consts, 1)
            pe.wait_ge(wa_done, 5)
            graph_steps(pe, step)

            pe.wait_ge(rest_in, 16 * REST)
            pe.transpose(bank[6][:, 0:E * MT], b1n[:, :], idf[0:E * MT, 0:E * MT]).then_inc(b1t_ps, 1)
            pe.wait_ge(macc_done, B)
            pe.matmul(bank[2][:, 0:E], ones16[:, :], macc[:, :], start=True, stop=True).then_inc(cnt_ps, 1)

            def transpose_rows(t, s):
                pe.wait_ge(xs_in[s], 16 * ((t - s) // 2 + 1) if isinstance(t, int) else t * 8 + (16 - 8 * s))
                wait(pe, xlo_done, t - 1)
                for k in range(KC):
                    for j in range(JT):
                        i_ = pe.transpose(bank[s][:, (k * JT + j) * P:(k * JT + j + 1) * P], xs[s][:, j, k * P:(k + 1) * P], idf[:, :])
                i_.then_inc(xst_ps, 1)

            def hidden(t, s, e):
                pe.wait_ge(xlo_done, t + 1)
                for m in range(FA):
                    wait(pe, act_done, FA * t - FA + m + 1 if not isinstance(t, int) or t > 0 else 0)
                    for half in range(2):
                        o = bank[2 + m][:, half * T:(half + 1) * T]
                        f = (half * FA + m) * P
                        terms = [(w1h, 0, 0), (w1h, 0, 1), (w1l, 0, 0)]
                        n_ = 0
                        for w, _, h in terms:
                            for k in range(KC):
                                i_ = pe.matmul(o, w[:, e * KC + k, f:f + P], xsT[s][:, h * KC + k, :],
                                               start=(n_ == 0), stop=(n_ == 3 * KC - 1))
                                n_ += 1
                    i_.then_inc(ag_ps, 1)

            def results(t, s, e):
                pe.wait_ge(al_done, FA * t + FA)
                wait(pe, yb_done, t - 1)
                for j in range(JT):
                    n_ = 0
                    for k in range(KF):
                        for a, w in ((ah, w2h), (ah, w2l), (al, w2h)):
                            i_ = pe.matmul(bank[6 + s][:, j * C:(j + 1) * C], a[s][:, k, j * P:(j + 1) * P],
                                           w[:, e * KF + k, :], start=(n_ == 0), stop=(n_ == 3 * KF - 1))
                            n_ += 1
                i_.then_inc(y_ps, 1)

            def expert(t):
                return pe.value_load(tabe[0:1, bass.ds(t, 1)], min_val=0, max_val=E - 1)

            pe.wait_ge(table, 3)
            e_0 = expert(0)
            transpose_rows(0, 0)
            hidden(0, 0, e_0)
            transpose_rows(1, 1)
            hidden(1, 1, expert(1))
            transpose_rows(2, 0)
            results(0, 0, expert(0))
            hidden(2, 0, expert(2))
            transpose_rows(3, 1)
            results(1, 1, expert(1))
            with pe.Fori(1, (NT - 3) // 2) as j:
                hidden(2 * j + 1, 1, expert(2 * j + 1))
                transpose_rows(2 * j + 2, 0)
                results(2 * j, 0, expert(2 * j))
                hidden(2 * j + 2, 0, expert(2 * j + 2))
                transpose_rows(2 * j + 3, 1)
                results(2 * j + 1, 1, expert(2 * j + 1))
            t = NT - 3
            hidden(t + 1, 1, expert(t + 1))
            transpose_rows(t + 2, 0)
            results(t, 0, expert(t))
            hidden(t + 2, 0, expert(t + 2))
            results(t + 1, 1, expert(t + 1))
            results(t + 2, 0, expert(t + 2))

        @block.scalar
        def _(sc):
            act_ = nc.scalar.activation
            sc.dma_start(wx[:, :, 0:C], gW.rearrange("(k p) f -> p k f", p=P)).then_inc(gnn_in, 16)
            sc.dma_start(betat[:, :], gbeta.partition_broadcast(P)).then_inc(gnn_in, 16)

            def step(G):
                for t in range(NI):
                    if m := tile_at(G, t, 1):
                        probs(*m)
                    if t < NI - 1 and G[1]:
                        plus_s1(G[1], t + 1)
                    if t == NI - 1 and G[0]:
                        plus_s1(G[0], 0)
                    if m := tile_at(G, t, 2):
                        probs_t(*m)
                    if t == 0 and G[0]:
                        normalise(*G[0])
                    if t == 1 and G[4]:
                        q, s = G[4]
                        sc.wait_ge(d_done, 2 * q + s + 1)
                        act_(meta(xn2[s], ED), meta(xn2[s], ED), ACT.Exp).then_inc(ed_done, 1)
                    if t == (1 if G[4] else 2) and G[0]:
                        whi(2 * G[0][0] + G[0][1])
                    if t == 1 and G[0]:
                        q, s = G[0]
                        b = 2 * q + s
                        for k in range(KC):
                            sc.wait_ge(t1_done, KC * b + k + 1)
                            wait(sc, s2_ps, b)
                            act_(xT[:, k, :], bank[k][:, :], ACT.Copy).then_inc(xT_sb, 1)
                    if t == 3 and G[2]:
                        q, s = G[2]
                        b = 2 * q + s
                        sc.wait_ge(z_done, NI * b + NI)
                        wait(sc, x1_done, b)
                        act_(ez[:, :, :], zb[s][:, :, :], ACT.Exp, bias=onesf[:, 0:1]).then_inc(ez_done, 1)
                    if t == 3 and G[3]:
                        q, s = G[3]
                        b = 2 * q + s
                        for k in range(KC):
                            sc.wait_ge(t2_done, KC * b + k + 1)
                            wait(sc, gate_done, b)
                            act_(x2T[:, k, :], bank[k][:, :], ACT.Copy).then_inc(x2T_sb, 1)
                    if t >= 2 and G[0]:
                        q, s = G[0]
                        b = 2 * q + s
                        for n in range(2 * t - 4, 2 * t - 2):
                            sc.wait_ge(h_ps, NI * b + n + 1)
                            if n == 0:
                                wait(sc, att_ps, NI * (b - 1))
                                wait(sc, bh_done, b - 1)
                            act_(hs[s][:, n, :], bank[3 + n % 2][:, 0:C + 1], ACT.Copy).then_inc(h_sb, 1)

            def normalise(q, s):
                b = 2 * q + s
                sc.wait_ge(nm1_done, b + 1)
                wait(sc, t1_done, KC * b)
                for n in range(NI):
                    act_(xn[:, n, :], xt[s][:, n, :], ACT.Identity, bias=nm1[:, n:n + 1], scale=rs1[:, n:n + 1]).then_inc(xn_done, 1)

            def whi(b):
                sc.wait_ge(w_in, 32 * b + 32)
                sc.nop(nofuse=True)
                act_(w1h[:, b, :], wst1[:, :], ACT.Copy, scale=SW).then_inc(whi_done, 1)
                act_(w2h[:, bass.ds(b * KC, KC), :], wst2[:, :, :], ACT.Copy, scale=SW).then_inc(whi_done, 1)

            def plus_s1(mid, i):
                q, s = mid
                b = 2 * q + s
                g = NI * b + i
                sc.wait_ge(s2_ps, b + 1)
                sc.wait_ge(h_sb, NI * b + i + 1)
                wait(sc, em_done, g - 1)
                act_(at_s[i % 2][:, :], bank[2][:, :], ACT.Identity, bias=hs[s][:, i, C:C + 1]).then_inc(a_done, 1)

            def probs(mid, i):
                q, s = mid
                g = NI * (2 * q + s) + i
                sc.wait_ge(nm_done, g + 1)
                wait(sc, ri_done, g - 3)
                wait(sc, pt_ps, g - 1)
                act_(pb[i % 2][:, :], em[i % 2][:, :], ACT.Exp, bias=nmax[:, i % 2, :], accum_out=rsum[:, i, :]).then_inc(p_done, 1)

            def probs_t(mid, i):
                q, s = mid
                g = NI * (2 * q + s) + i
                sc.wait_ge(pt_ps, g + 1)
                wait(sc, att_ps, g - 1)
                act_(pT[i % 2][:, :, :], bank[5 + i % 2][:, :].rearrange("p (j r) -> p j r", j=NI), ACT.Copy).then_inc(pt_sb, 1)

            sc.wait_ge(onesd, 1)
            act_(warm[:, :], warm[:, :], ACT.Exp)
            graph_steps(sc, step)

            act_(warm[:, :], warm[:, :], ACT.Silu)
            sc.wait_ge(table, 3)
            sc.wait_ge(b1t_sb, 2)

            def rows_high(t, s):
                sc.wait_ge(xst_ps, t + 1)
                wait(sc, ag_ps, FA * (t - 1))
                act_(xsT[s][:, 0:KC, :].rearrange("p c r -> p (c r)"), bank[s][:, :], ACT.Copy).then_inc(xhi_done, 1)

            def tile(t, s, more=True):
                e = sc.value_load(tabe[0:1, bass.ds(t, 1)], min_val=0, max_val=E - 1)
                for m in range(FA):
                    sc.wait_ge(ag_ps, FA * t + m + 1)
                    wait(sc, act_done, FA * t + m - 1)
                    sc.nop(nofuse=True)
                    act_(sil[m % 2][:, :], bank[2 + m][:, 0:T], ACT.Silu, bias=b1T[:, bass.ds(e * MT + m, 1)],
                         scale=1.0 / (SX * SW)).then_inc(sil_done, 1)
                    if m == FA - 1 and more:
                        rows_high(t + 1, 1 - s)
                    if m >= 1:
                        high(t, s, m - 1)
                high(t, s, FA - 1)

            def high(t, s, m):
                sc.wait_ge(act_done, FA * t + m + 1)
                if m == 0:
                    wait(sc, y_ps, t - 1)
                act_(ah[s][:, m, :], act[m % 2][:, :], ACT.Copy, scale=SA / (SX * SW)).then_inc(ah_done, 1)

            rows_high(0, 0)
            tile(0, 0)
            tile(1, 1)
            with sc.Fori(1, (NT - 1) // 2) as j:
                tile(2 * j, 0)
                tile(2 * j + 1, 1)
            tile(NT - 1, 0, more=False)

        @block.vector
        def _(ve):
            def moments1(q, s):
                b = 2 * q + s
                ve.wait_ge(x_in[s], 16 * q + 16)
                wait(ve, rs1_done, b)
                for n in range(NI):
                    ve.bn_stats(st1[:, n, :], xt[s][:, n, :]).then_inc(ln1_st, 1)

            def moments1_end(q, s):
                ve.wait_ge(ln1_st, NI * (2 * q + s) + NI)
                ve.nop(nofuse=True)
                for n in range(NI):
                    ve.bn_aggr(mv1[:, n, :], st1[:, n, :]).then_inc(ln1_mv, 1)

            moments1(0, 0)
            moments1_end(0, 0)
            ve.wait_ge(gnn_in, 16 * 3)
            for k in range(KC):
                ve.tensor_tensor_reduce(ez[:, k, :], wx[:, k, 0:C], av[:, 0:C], 1.0, 0.0, ALU.mult, ALU.add, wx[:, k, C:C + 1]).then_inc(wa_done, 1)
                ve.tensor_tensor_reduce(ez[:, 2 + k, :], wx[:, k, 0:C], av[:, C:2 * C], 1.0, 0.0, ALU.mult, ALU.add, wa2[:, k:k + 1]).then_inc(wa_done, 1)
            ve.wait_ge(wa_done, 4)
            ve.wait_ge(onesd, 5)
            for k in range(KC):
                i_ = ve.tensor_scalar(wa2r[:, k, :], onesf[:, :], wa2[:, k:k + 1], None, ALU.mult)
            i_.then_inc(wa_done, 1)

            def step(G):
                for t in range(NI):
                    if t == 3 and G[4] and not late(G):
                        ranked(G[4], rank_ps[0])
                    if t == 0 and G[0]:
                        shift(*G[0])
                    if m := tile_at(G, t, 4):
                        attended(*m)
                    if t == 2 and G[4] and late(G):
                        ranked(G[4], rank_ps[1])
                    if t == 1 and G[4]:
                        logits(G[4])
                    if t == 3 and next_graph(G):
                        moments1_end(*next_graph(G))
                    if G[1]:
                        leaky(G[1], t)
                    if t == 1 and G[4]:
                        maxima(G[4])
                    if t == (2 if late(G) else 3) and G[4]:
                        slots(G[4])
                    if t == 0 and G[3]:
                        x1(*G[3])
                    if G[1]:
                        scores(G[1], t)
                    if t == 1 and G[4]:
                        experts(G[4])
                    if t == 0 and G[3]:
                        moments2(*G[3])
                    if t == 2 and next_graph(G):
                        moments1(*next_graph(G))
                    if G[1]:
                        negate(G[1], t)
                    if t == 1 and G[4]:
                        choices(G[4])
                    if t == 0 and G[3]:
                        moments2_end(*G[3])
                    if t == 1 and G[4]:
                        one_hots(G[4])
                        chosen(G[4])
                    if t == 2 and G[3]:
                        normalise_x1(*G[3])
                    if t == 3 and G[2]:
                        q, s = G[2]
                        b = 2 * q + s
                        ve.wait_ge(xr_in[s], 16 * q + 16)
                        ve.wait_ge(z_done, NI * b + NI)
                        ve.scalar_tensor_tensor(xr[s][:, :, :], zb[s][:, :, :], -1.0, xr[s][:, :, :], ALU.max, ALU.add).then_inc(rl_done, 1)

            def shift(q, s):
                b = 2 * q + s
                ve.wait_ge(rs1_done, b + 1)
                wait(ve, xn_done, NI * b)
                ve.scalar_tensor_tensor(nm1[:, :], mv1[:, :, 0], -1.0, rs1[:, :], ALU.mult, ALU.mult).then_inc(nm1_done, 1)

            def normalise_x1(q, s):
                b = 2 * q + s
                ve.wait_ge(rs2_done, b + 1)
                wait(ve, t2_done, KC * (b - 1))
                wait(ve, scattered[s], 16 * 2 * NI * q)
                for n in range(NI):
                    ve.tensor_scalar(xn2[s][:, n, 0:C], xr[s][:, n, :], mv2[:, n, 0:1], rs2[:, n:n + 1], ALU.subtract, ALU.mult).then_inc(xn2_done, 1)

            def x1(q, s):
                b = 2 * q + s
                ve.wait_ge(ez_done, b + 1)
                ve.wait_ge(rl_done, b + 1)
                ve.scalar_tensor_tensor(xr[s][:, :, :], ez[:, :, :], 1.0, xr[s][:, :, :], ALU.min, ALU.add).then_inc(x1_done, 1)

            def moments2(q, s):
                b = 2 * q + s
                ve.wait_ge(x1_done, b + 1)
                wait(ve, rs2_done, b)
                for n in range(NI):
                    ve.bn_stats(st2[:, n, :], xr[s][:, n, :]).then_inc(ln2_st, 1)

            def moments2_end(q, s):
                ve.wait_ge(ln2_st, NI * (2 * q + s) + NI)
                ve.nop(nofuse=True)
                for n in range(NI):
                    ve.bn_aggr(mv2[:, n, :], st2[:, n, :]).then_inc(ln2_mv, 1)

            def leaky(mid, i):
                q, s = mid
                g = NI * (2 * q + s) + i
                ve.wait_ge(a_done, g + 1)
                ve.scalar_tensor_tensor(at_s[i % 2][:, :], at_s[i % 2][:, :], ALPHA, at_s[i % 2][:, :], ALU.mult, ALU.max).then_inc(lr_done, 1)

            def scores(mid, i):
                q, s = mid
                g = NI * (2 * q + s) + i
                ve.wait_ge(lr_done, g + 1)
                if isinstance(g, int) and g < NI:
                    ve.wait_ge(masked, i // 2 + 1)
                wait(ve, p_done, g - 1)
                ve.nop(nofuse=True)
                ve.tensor_tensor_reduce(em[i % 2][:, :], at_s[i % 2][:, :], mask[:, i, :], 1.0, -3.0e38, ALU.mult, ALU.max, rmax[:, i % 2, :]).then_inc(em_done, 1)

            def attended(mid, i):
                q, s = mid
                b = 2 * q + s
                g = NI * b + i
                ve.wait_ge(p_done, g + 1)
                wait(ve, z_done, g - 1)
                ve.reciprocal(rinv[:, i % 2, :], rsum[:, i, :]).then_inc(ri_done, 1)
                ve.wait_ge(ri_done, g + 1)
                ve.wait_ge(att_ps, g + 1)
                ve.wait_ge(bh_done, b + 1)
                ve.scalar_tensor_tensor(zb[s][:, i, :], bank[7][:, 0:C], rinv[:, i % 2, :],
                                        zb[s][:, i, :], ALU.mult, ALU.add).then_inc(z_done, 1)

            def negate(mid, i):
                q, s = mid
                g = NI * (2 * q + s) + i
                ve.wait_ge(em_done, g + 1)
                ve.tensor_scalar(nmax[:, i % 2, :], rmax[:, i % 2, :], -1.0, None, ALU.mult).then_inc(nm_done, 1)

            def logits(back):
                q, s = back
                b = 2 * q + s
                if isinstance(b, int) and b == 0:
                    ve.wait_ge(rest_in, 16 * REST)
                ve.wait_ge(gate_done, b + 1)
                ve.scalar_tensor_tensor(lg[:, :, :], gate_ps.rearrange("p (n e) -> p n e", e=E), 1.0 / SX, bgb[:, :, :], ALU.mult, ALU.add).then_inc(lg_done, 1)

            def maxima(back):
                q, s = back
                ve.wait_ge(lg_done, 2 * q + s + 1)
                ve.nop(nofuse=True)
                for n in range(NI):
                    ve.max(mx[:, n, :], lg[:, n, :]).then_inc(mx_done, 1)

            def experts(back):
                q, s = back
                b = 2 * q + s
                ve.wait_ge(mx_done, NI * b + NI)
                ve.nop(nofuse=True)
                for n in range(NI):
                    ve.max_index(ix[:, n, :], mx[:, n, :], lg[:, n, :]).then_inc(ix_done, 1)
                ve.tensor_tensor(meta(xn2[s], ED), mx[:, :, 1], mx[:, :, 0], ALU.subtract).then_inc(d_done, 1)

            def choices(back):
                q, s = back
                b = 2 * q + s
                ve.wait_ge(ix_done, NI * b + NI)
                ve.tensor_copy(ixf[:, :, :], ix[:, :, 0:2].rearrange("p n k -> p k n")).then_inc(ixf_done, 1)

            def one_hots(back):
                q, s = back
                b = 2 * q + s
                ve.wait_ge(ixf_done, b + 1)
                ve.tensor_tensor(oh[:, :, :], iota2[:, :, :], ixf[:, :, :].rearrange("p k n -> p (k n)").unsqueeze(2).broadcast_to((P, 2 * NI, E)), ALU.is_equal).then_inc(oh_done, 1)

            def chosen(back):
                q, s = back
                b = 2 * q + s
                ve.wait_ge(oh_done, b + 1)
                wait(ve, rank_done, b)
                ve.tensor_tensor(m16[:, :, :], oh[:, 0:NI, :], oh[:, NI:2 * NI, :], ALU.add).then_inc(m_done, 1)

            def ranked(back, ps):
                q, s = back
                b = 2 * q + s
                ve.wait_ge(m_done, b + 1)
                ve.tensor_reduce(msum[:, :], m16[:, :, :].rearrange("p n e -> p e n"), AX, ALU.add).then_inc(msum_done, 1)
                ve.wait_ge(rank_done, b + 1)
                if ps is rank_ps[0]:
                    ve.wait_ge(att_ps, min(NI * (b + 3), NI * B) if isinstance(b, int) else NI * (b + 3))
                for k in range(2):
                    i_ = ve.tensor_tensor(rk[:, k * NI:(k + 1) * NI, :], oh[:, k * NI:(k + 1) * NI, :],
                                          ps.rearrange("p (n e) -> p n e", e=E), ALU.mult)
                i_.then_inc(rk_done, 1)

            def slots(back):
                q, s = back
                b = 2 * q + s
                ve.wait_ge(rk_done, b + 1)
                ve.tensor_reduce(rkr[:, :], rk[:, :, :], AX, ALU.add).then_inc(rkr_done, 1)
                ve.wait_ge(msum_done, b + 1)
                ve.tensor_tensor(macc[:, :], macc[:, :], msum[:, :], ALU.add).then_inc(macc_done, 1)
                ve.tensor_copy(meta(xn2[s], TOKEN, I32), tokc[s][:, :])
                ve.tensor_copy(meta(xn2[s], E0), ixf[:, 0, :])
                ve.tensor_scalar(tokc[s][:, :], tokc[s][:, :], float(2 * N), None, ALU.add)
                ve.wait_ge(rkr_done, b + 1)
                wait(ve, scattered[s], 16 * 2 * NI * q)
                ve.scalar_tensor_tensor(slot[s][:, :], ixf[:, :, :].rearrange("p k n -> p (k n)"), float(R), rkr[:, :], ALU.mult, ALU.add).then_inc(slot_done, 1)

            ve.wait_ge(consts, 2)
            ve.tensor_copy(ones16[:, :], onesf[:, :])
            ve.tensor_copy(tri[:, :], trif[:, :]).then_inc(wa_done, 1)
            graph_steps(ve, step, tail=2)

            n_ = 0

            def then(i_):
                nonlocal n_
                i_.then_inc(tb, 1)
                n_ += 1
                ve.wait_ge(tb, n_)

            ve.wait_ge(cnt_ps, 1)
            then(ve.tensor_copy(cnt[:, :], bank[2][:, 0:E]))
            ve.tensor_copy(cnti[:, :], cnt[:, :]).then_inc(table, 1)
            ve.memset(one8[:, :], 1.0)
            then(ve.tensor_scalar(cntp[:, :], cnt[:, :], float(T - 1), None, ALU.add))
            then(ve.tensor_scalar(nti[:, :], cntp[:, :], T.bit_length() - 1, None, ALU.logical_shift_right))
            then(ve.tensor_copy(ntf[:, :], nti[:, :]))
            then(ve.tensor_tensor_scan(ends[:, :], one8[:, :], ntf[:, :], 0.0, ALU.mult, ALU.add))
            then(ve.tensor_tensor(ge[:, :, :], s_io[:, :].unsqueeze(2).broadcast_to((P, NT, E)), ends[:, :].unsqueeze(1).broadcast_to((P, NT, E)), ALU.is_ge))
            ve.tensor_reduce(ex[:, :], ge[:, :, :], AX, ALU.add)
            then(ve.tensor_tensor(gn[:, :, :], ge[:, :, :], ntf[:, :].unsqueeze(1).broadcast_to((P, NT, E)), ALU.mult))
            then(ve.tensor_reduce(stt[:, :], gn[:, :, :], AX, ALU.add))
            ve.tensor_scalar(tabe[:, :], ex[:, :], float(E - 1), None, ALU.min)
            then(ve.tensor_tensor(srow[:, :], s_io[:, :], stt[:, :], ALU.subtract))
            then(ve.tensor_scalar(srow[:, :], srow[:, :], float(T), None, ALU.mult))
            then(ve.scalar_tensor_tensor(srow[:, :], ex[:, :], float(R), srow[:, :], ALU.mult, ALU.add))
            then(ve.tensor_scalar(tabr[:, :], srow[:, :], float(E * R), None, ALU.min))
            ve.nop().then_inc(table, 2)
            ve.wait_ge(b1t_ps, 1)
            ve.tensor_copy(b1T[:, :], bank[6][:, 0:E * MT]).then_inc(b1t_sb, 1)
            ve.tensor_scalar(b1S[:, :], bank[6][:, 0:E * MT], SX * SW, None, ALU.mult).then_inc(b1t_sb, 1)
            ve.wait_ge(b1t_sb, 2)

            def rows_low(t, s):
                ve.wait_ge(xhi_done, t + 1)
                wait(ve, ag_ps, FA * (t - 1))
                ve.tensor_tensor(xsT[s][:, KC:2 * KC, :].rearrange("p c r -> p (c r)"), bank[s][:, :], xsT[s][:, 0:KC, :].rearrange("p c r -> p (c r)"), ALU.subtract).then_inc(xlo_done, 1)

            def tile(t, s, more=True):
                e = ve.value_load(tabe[0:1, bass.ds(t, 1)], min_val=0, max_val=E - 1)
                for m in range(FA):
                    ve.wait_ge(sil_done, FA * t + m + 1)
                    wait(ve, ah_done, FA * t + m - 1)
                    wait(ve, al_done, FA * t + m - 1)
                    ve.scalar_tensor_tensor(act[m % 2][:, :], bank[2 + m][:, T:2 * T], b1S[:, bass.ds(e * MT + FA + m, 1)],
                                            sil[m % 2][:, :], ALU.add, ALU.mult).then_inc(act_done, 1)
                    if m == FA - 1 and more:
                        rows_low(t + 1, 1 - s)
                    if m >= 1:
                        low(t, s, m - 1)
                low(t, s, FA - 1)
                row_weights(t, s)

            def row_weights(t, s):
                wait(ve, added[s], added_before(t, s))
                ve.tensor_copy(tok[s][:, :], meta(xs[s], TOKEN, I32))
                ve.tensor_scalar(wden[:, :], meta(xs[s], ED), 1.0, None, ALU.add).then_inc(wm, 1)
                ve.scalar_tensor_tensor(wsel[:, :], meta(xs[s], E0), ex[:, bass.ds(t, 1)], meta(xs[s], ED), ALU.is_equal, ALU.max).then_inc(wm, 1)
                ve.wait_ge(wm, 3 * t + 2)
                ve.reciprocal(winv[:, :], wden[:, :]).then_inc(wm, 1)
                ve.wait_ge(wm, 3 * t + 3)
                ve.tensor_tensor(wrow[s][:, :], wsel[:, :], winv[:, :], ALU.mult).then_inc(wrow_done, 1)

            def added_before(t, s):
                return 16 * JT * ((t - s) // 2) if isinstance(t, int) else t * (8 * JT) - 8 * JT * s

            def low(t, s, m):
                ve.wait_ge(ah_done, FA * t + m + 1)
                ve.wait_ge(act_done, FA * t + m + 1)
                ve.scalar_tensor_tensor(al[s][:, m, :], act[m % 2][:, :], SA / (SX * SW), ah[s][:, m, :], ALU.mult, ALU.subtract).then_inc(al_done, 1)

            def result(t, s):
                e = ve.value_load(tabe[0:1, bass.ds(t, 1)], min_val=0, max_val=E - 1)
                ve.wait_ge(y_ps, t + 1)
                wait(ve, added[s], added_before(t, s))
                ve.scalar_tensor_tensor(ys[s][:, :, :], bank[6 + s][:, :].rearrange("p (j c) -> p j c", j=JT), 1.0 / (SA * SW),
                                        b2b[:, bass.ds(e, 1), :].broadcast_to((P, JT, C)), ALU.mult, ALU.add).then_inc(yb_done, 1)
                ve.wait_ge(yb_done, t + 1)
                ve.wait_ge(wrow_done, t + 1)
                for j in range(JT):
                    i_ = ve.tensor_scalar(ys[s][:, j, :], ys[s][:, j, :], wrow[s][:, j:j + 1], None, ALU.mult)
                i_.then_inc(y_sb, 1)

            rows_low(0, 0)
            tile(0, 0)
            tile(1, 1)
            result(0, 0)
            tile(2, 0)
            result(1, 1)
            tile(3, 1)
            result(2, 0)
            with ve.Fori(2, (NT - 1) // 2) as j:
                tile(2 * j, 0)
                result(2 * j - 1, 1)
                tile(2 * j + 1, 1)
                result(2 * j, 0)
            tile(NT - 1, 0, more=False)
            result(NT - 2, 1)
            result(NT - 1, 0)


_INS = ['x', 'adj', 'L0_gnn_W', 'L0_gnn_a', 'L0_gnn_beta', 'L0_ffn_Wg', 'L0_ffn_bg', 'L0_ffn_W1', 'L0_ffn_b1', 'L0_ffn_W2', 'L0_ffn_b2']
_OUT = (16, 512, 256)


def kernel(**inputs):
    import numpy as _np
    import concourse.bacc as _bacc
    from concourse import mybir as _mybir
    from concourse.bass_utils import run_bass_kernel_spmd as _run

    nc = _bacc.Bacc("TRN2", target_bir_lowering=False, num_devices=1)
    arrays, args = {}, []
    for name in _INS:
        a = _np.ascontiguousarray(inputs[name])
        arrays[f"in_{name}_dram"] = a
        args.append(nc.dram_tensor(f"in_{name}_dram", a.shape, _mybir.dt.from_np(a.dtype), kind="ExternalInput").ap())
    b, n, c = _OUT
    args.append(nc.dram_tensor("out_dram", (b * n + T, c), _mybir.dt.float32, kind="ExternalOutput").ap())
    build_gat_moe(nc, *args)
    r = _run(nc, [arrays], core_ids=[0])
    return r.results[0]["out_dram"][:b * n].reshape(_OUT)
```
